# Optimizing a Trainium2 kernel written in Bass

```python
import numpy as np
import jax
import jax.numpy as jnp

def _softmax(x, axis=-1):
    return jax.nn.softmax(x, axis=axis)

def _gelu(x):
    return jax.nn.gelu(x, approximate=True)

def _silu(x):
    return jax.nn.silu(x)

def _sigmoid(x):
    return jax.nn.sigmoid(x)

def _layernorm(x, axis=-1, eps=1e-05):
    m = jnp.mean(x, axis=axis, keepdims=True)
    v = jnp.var(x, axis=axis, keepdims=True)
    return (x - m) / jnp.sqrt(v + eps)

def _scatter_add(tgt, idx, src, axis=0):
    return tgt.at[idx].add(src)

def _segment_sum(src, seg, n):
    return jax.ops.segment_sum(src, seg, n)
kernel_name = 'mk_prb_d1_jaxref_r8_33caee'

def setup_inputs(seed: int=0):
    np.random.seed(seed)
    _w = jnp.asarray

    def _L0_attn_setup():
        import jax, jax.numpy as jnp
        import numpy as np
        N_HEADS = 16
        key = jax.random.key(seed)
        ks = jax.random.split(key, 8)
        B, T, D = (2, 256, 128)
        hd, rank = (D // N_HEADS, 32)
        std = 0.02
        inp = {'x': jax.random.normal(ks[0], (B, T, D), jnp.float32), 'Wq': jax.random.normal(ks[1], (D, D), jnp.float32) * std, 'bq': jnp.zeros((D,), jnp.float32), 'Wk': jax.random.normal(ks[2], (D, D), jnp.float32) * std, 'bk': jnp.zeros((D,), jnp.float32), 'Wv': jax.random.normal(ks[3], (D, D), jnp.float32) * std, 'bv': jnp.zeros((D,), jnp.float32), 'Wo': jax.random.normal(ks[4], (D, D), jnp.float32) * std, 'bo': jnp.zeros((D,), jnp.float32), 'U': jnp.linalg.qr(jax.random.normal(ks[5], (hd, rank), jnp.float32))[0], 'V': jnp.linalg.qr(jax.random.normal(ks[6], (hd, rank), jnp.float32))[0]}
        return inp
    _L0_attn_in = _L0_attn_setup()

    def _L0_ffn_setup():
        import jax, jax.numpy as jnp
        import numpy as np
        DIM = 128
        DEPTH = 6
        HEADS = 16
        DIM_HEAD = 64
        WINDOW = 32
        INNER = HEADS * DIM_HEAD
        DIM_INNER = int(DIM * 4 * 2 / 3)
        QK_SCALE = 8.0

        def shift_tokens(t):
            a, s = jnp.split(t, 2, -1)
            s = jnp.pad(s, ((0, 0), (1, 0), (0, 0)))[:, :-1]
            return jnp.concatenate([a, s], -1)

        def l2norm(t):
            return t / jnp.maximum(jnp.linalg.norm(t, axis=-1, keepdims=True), 1e-12)

        def rotate_half(x):
            x1, x2 = jnp.split(x, 2, -1)
            return jnp.concatenate([-x2, x1], -1)

        def rotary_tables(n):
            half = jnp.arange(0, DIM_HEAD, 2, dtype=jnp.float32)
            inv_freq = 1.0 / 10000.0 ** (half / DIM_HEAD)
            t = jnp.arange(n, dtype=jnp.float32)
            freqs = t[:, None] * inv_freq[None, :]
            freqs = jnp.concatenate([freqs, freqs], -1)
            base_scale = (half + 0.4 * DIM_HEAD) / (1.4 * DIM_HEAD)
            power = (t - n // 2) / (WINDOW // 2)
            scale = base_scale[None, :] ** power[:, None]
            scale = jnp.concatenate([scale, scale], -1)
            return (freqs, scale)

        def local_attention(q, k, v):
            b, h, n, d = q.shape
            w = WINDOW
            nw = n // w
            bq = q.reshape(b, h, nw, w, d)
            bk = k.reshape(b, h, nw, w, d)
            bv = v.reshape(b, h, nw, w, d)

            def look(t):
                p = jnp.pad(t, ((0, 0), (0, 0), (1, 0), (0, 0), (0, 0)))
                return jnp.concatenate([p[:, :, :nw], p[:, :, 1:]], axis=3)
            bk2, bv2 = (look(bk), look(bv))
            seq = jnp.arange(n).reshape(nw, w)
            seq_p = jnp.pad(seq, ((1, 0), (0, 0)), constant_values=-1)
            jt = jnp.concatenate([seq_p[:nw], seq_p[1:]], axis=1)
            it = seq[:, :, None]
            jb = jt[:, None, :]
            mask = (it < jb) | (it > jb + w) | (jb == -1)
            sim = jnp.einsum('bhwie,bhwje->bhwij', bq, bk2) * QK_SCALE
            sim = jnp.where(mask, -jnp.finfo(sim.dtype).max, sim)
            attn = jax.nn.softmax(sim, -1)
            out = jnp.einsum('bhwij,bhwje->bhwie', attn, bv2)
            return out.reshape(b, h, n, d)

        def attn_layer(x, Wqkv, qs, ksc, Wo):
            b, n, _ = x.shape
            qkv = x @ Wqkv
            q, k, v = jnp.split(qkv, 3, -1)
            sh = lambda t: t.reshape(b, n, HEADS, DIM_HEAD).transpose(0, 2, 1, 3)
            q, k, v = (sh(q), sh(k), sh(v))
            q = l2norm(q) * qs
            k = l2norm(k) * ksc
            freqs, scale = rotary_tables(n)
            cos, sin = (jnp.cos(freqs), jnp.sin(freqs))
            q = q * cos * scale + rotate_half(q) * sin * scale
            inv = 1.0 / scale
            k = k * cos * inv + rotate_half(k) * sin * inv
            out = local_attention(q, k, v)
            out = out.transpose(0, 2, 1, 3).reshape(b, n, INNER)
            return out @ Wo

        def ffn_layer(x, g, bln, W1, b1, W2, b2):
            mu = x.mean(-1, keepdims=True)
            var = ((x - mu) ** 2).mean(-1, keepdims=True)
            xn = (x - mu) / jnp.sqrt(var + 1e-05) * g + bln
            hg = xn @ W1 + b1
            a, gate = jnp.split(hg, 2, -1)
            return a * jax.nn.gelu(gate, approximate=False) @ W2 + b2
        key = jax.random.key(seed)
        ks = jax.random.split(key, 8)
        B, N = (2, 256)
        init = lambda k, shape: jax.random.normal(k, shape, jnp.float32) * 0.02
        return {'x': jax.random.normal(ks[0], (B, N, DIM), jnp.float32), 'Wqkv': init(ks[1], (DEPTH, DIM, 3 * INNER)), 'q_scale': jnp.ones((DEPTH, DIM_HEAD), jnp.float32), 'k_scale': jnp.ones((DEPTH, DIM_HEAD), jnp.float32), 'Wo': init(ks[2], (DEPTH, INNER, DIM)), 'ln_g': jnp.ones((DEPTH, DIM), jnp.float32), 'ln_b': jnp.zeros((DEPTH, DIM), jnp.float32), 'W1': init(ks[3], (DEPTH, DIM, 2 * DIM_INNER)), 'b1': jnp.zeros((DEPTH, 2 * DIM_INNER), jnp.float32), 'W2': init(ks[4], (DEPTH, DIM_INNER, DIM)), 'b2': jnp.zeros((DEPTH, DIM), jnp.float32)}
    _L0_ffn_in = _L0_ffn_setup()
    _d = {'L0_attn_x': _L0_attn_in['x'], 'L0_attn_Wq': _L0_attn_in['Wq'], 'L0_attn_bq': _L0_attn_in['bq'], 'L0_attn_Wk': _L0_attn_in['Wk'], 'L0_attn_bk': _L0_attn_in['bk'], 'L0_attn_Wv': _L0_attn_in['Wv'], 'L0_attn_bv': _L0_attn_in['bv'], 'L0_attn_Wo': _L0_attn_in['Wo'], 'L0_attn_bo': _L0_attn_in['bo'], 'L0_attn_U': _L0_attn_in['U'], 'L0_attn_V': _L0_attn_in['V'], 'L0_ffn_Wqkv': _L0_ffn_in['Wqkv'], 'L0_ffn_q_scale': _L0_ffn_in['q_scale'], 'L0_ffn_k_scale': _L0_ffn_in['k_scale'], 'L0_ffn_Wo': _L0_ffn_in['Wo'], 'L0_ffn_ln_g': _L0_ffn_in['ln_g'], 'L0_ffn_ln_b': _L0_ffn_in['ln_b'], 'L0_ffn_W1': _L0_ffn_in['W1'], 'L0_ffn_b1': _L0_ffn_in['b1'], 'L0_ffn_W2': _L0_ffn_in['W2'], 'L0_ffn_b2': _L0_ffn_in['b2']}
    _x0 = _d['L0_attn_x']
    _d['L0_attn_x'] = jax.random.normal(jax.random.fold_in(jax.random.key(seed), 1), (1, 2048, 128), dtype=_x0.dtype)
    del _x0
    return _d

def reference(L0_attn_x, L0_attn_Wq, L0_attn_bq, L0_attn_Wk, L0_attn_bk, L0_attn_Wv, L0_attn_bv, L0_attn_Wo, L0_attn_bo, L0_attn_U, L0_attn_V, L0_ffn_Wqkv, L0_ffn_q_scale, L0_ffn_k_scale, L0_ffn_Wo, L0_ffn_ln_g, L0_ffn_ln_b, L0_ffn_W1, L0_ffn_b1, L0_ffn_W2, L0_ffn_b2):

    def _L0_attn_ref(x, Wq, bq, Wk, bk, Wv, bv, Wo, bo, U, V):
        import jax, jax.numpy as jnp
        import numpy as np
        N_HEADS = 16
        B, T, D = x.shape
        H = N_HEADS
        hd = D // H
        rank = V.shape[1]
        q = (x @ Wq.T + bq).reshape(B, T, H, hd).transpose(0, 2, 1, 3)
        k = (x @ Wk.T + bk).reshape(B, T, H, hd).transpose(0, 2, 1, 3)
        v = (x @ Wv.T + bv).reshape(B, T, H, hd).transpose(0, 2, 1, 3)
        zq = q @ V
        zk = k @ V
        zv = v @ V
        att = jnp.einsum('bhqr,bhkr->bhqk', zq, zk) / jnp.sqrt(jnp.float32(max(rank, 1)))
        att = jax.nn.softmax(att, axis=-1)
        y_r = jnp.einsum('bhqk,bhkr->bhqr', att, zv)
        y = y_r @ U.T
        y = y.transpose(0, 2, 1, 3).reshape(B, T, D)
        return y @ Wo.T + bo

    def _L0_ffn_ref(x, Wqkv, q_scale, k_scale, Wo, ln_g, ln_b, W1, b1, W2, b2):
        import jax, jax.numpy as jnp
        import numpy as np
        DIM = 128
        DEPTH = 6
        HEADS = 16
        DIM_HEAD = 64
        WINDOW = 32
        INNER = HEADS * DIM_HEAD
        DIM_INNER = int(DIM * 4 * 2 / 3)
        QK_SCALE = 8.0

        def shift_tokens(t):
            a, s = jnp.split(t, 2, -1)
            s = jnp.pad(s, ((0, 0), (1, 0), (0, 0)))[:, :-1]
            return jnp.concatenate([a, s], -1)

        def l2norm(t):
            return t / jnp.maximum(jnp.linalg.norm(t, axis=-1, keepdims=True), 1e-12)

        def rotate_half(x):
            x1, x2 = jnp.split(x, 2, -1)
            return jnp.concatenate([-x2, x1], -1)

        def rotary_tables(n):
            half = jnp.arange(0, DIM_HEAD, 2, dtype=jnp.float32)
            inv_freq = 1.0 / 10000.0 ** (half / DIM_HEAD)
            t = jnp.arange(n, dtype=jnp.float32)
            freqs = t[:, None] * inv_freq[None, :]
            freqs = jnp.concatenate([freqs, freqs], -1)
            base_scale = (half + 0.4 * DIM_HEAD) / (1.4 * DIM_HEAD)
            power = (t - n // 2) / (WINDOW // 2)
            scale = base_scale[None, :] ** power[:, None]
            scale = jnp.concatenate([scale, scale], -1)
            return (freqs, scale)

        def local_attention(q, k, v):
            b, h, n, d = q.shape
            w = WINDOW
            nw = n // w
            bq = q.reshape(b, h, nw, w, d)
            bk = k.reshape(b, h, nw, w, d)
            bv = v.reshape(b, h, nw, w, d)

            def look(t):
                p = jnp.pad(t, ((0, 0), (0, 0), (1, 0), (0, 0), (0, 0)))
                return jnp.concatenate([p[:, :, :nw], p[:, :, 1:]], axis=3)
            bk2, bv2 = (look(bk), look(bv))
            seq = jnp.arange(n).reshape(nw, w)
            seq_p = jnp.pad(seq, ((1, 0), (0, 0)), constant_values=-1)
            jt = jnp.concatenate([seq_p[:nw], seq_p[1:]], axis=1)
            it = seq[:, :, None]
            jb = jt[:, None, :]
            mask = (it < jb) | (it > jb + w) | (jb == -1)
            sim = jnp.einsum('bhwie,bhwje->bhwij', bq, bk2) * QK_SCALE
            sim = jnp.where(mask, -jnp.finfo(sim.dtype).max, sim)
            attn = jax.nn.softmax(sim, -1)
            out = jnp.einsum('bhwij,bhwje->bhwie', attn, bv2)
            return out.reshape(b, h, n, d)

        def attn_layer(x, Wqkv, qs, ksc, Wo):
            b, n, _ = x.shape
            qkv = x @ Wqkv
            q, k, v = jnp.split(qkv, 3, -1)
            sh = lambda t: t.reshape(b, n, HEADS, DIM_HEAD).transpose(0, 2, 1, 3)
            q, k, v = (sh(q), sh(k), sh(v))
            q = l2norm(q) * qs
            k = l2norm(k) * ksc
            freqs, scale = rotary_tables(n)
            cos, sin = (jnp.cos(freqs), jnp.sin(freqs))
            q = q * cos * scale + rotate_half(q) * sin * scale
            inv = 1.0 / scale
            k = k * cos * inv + rotate_half(k) * sin * inv
            out = local_attention(q, k, v)
            out = out.transpose(0, 2, 1, 3).reshape(b, n, INNER)
            return out @ Wo

        def ffn_layer(x, g, bln, W1, b1, W2, b2):
            mu = x.mean(-1, keepdims=True)
            var = ((x - mu) ** 2).mean(-1, keepdims=True)
            xn = (x - mu) / jnp.sqrt(var + 1e-05) * g + bln
            hg = xn @ W1 + b1
            a, gate = jnp.split(hg, 2, -1)
            return a * jax.nn.gelu(gate, approximate=False) @ W2 + b2
        for i in range(DEPTH):
            x = attn_layer(shift_tokens(x), Wqkv[i], q_scale[i], k_scale[i], Wo[i]) + x
            x = ffn_layer(shift_tokens(x), ln_g[i], ln_b[i], W1[i], b1[i], W2[i], b2[i]) + x
        return x
    x = L0_attn_x
    xn = _layernorm(x, axis=-1)
    x = x + _L0_attn_ref(xn, L0_attn_Wq, L0_attn_bq, L0_attn_Wk, L0_attn_bk, L0_attn_Wv, L0_attn_bv, L0_attn_Wo, L0_attn_bo, L0_attn_U, L0_attn_V) + _L0_ffn_ref(xn, L0_ffn_Wqkv, L0_ffn_q_scale, L0_ffn_k_scale, L0_ffn_Wo, L0_ffn_ln_g, L0_ffn_ln_b, L0_ffn_W1, L0_ffn_b1, L0_ffn_W2, L0_ffn_b2)
    return x

_drawn_inputs = setup_inputs


def setup_inputs(seed=0):
    import zlib

    import numpy as np

    out = dict(_drawn_inputs(seed))
    spreads = {'L0_attn_bq': (0.0, 0.8),
     'L0_attn_bk': (0.0, 2.0),
     'L0_attn_bv': (0.0, 0.77),
     'L0_attn_bo': (0.0, 0.8),
     'L0_ffn_q_scale': (1.0, 0.6),
     'L0_ffn_k_scale': (1.0, 0.6),
     'L0_ffn_ln_g': (1.0, 0.6),
     'L0_ffn_ln_b': (0.0, 0.8),
     'L0_ffn_b1': (0.0, 0.8),
     'L0_ffn_b2': (0.0, 0.8)}
    factors = {'L0_attn_Wq': 8.0,
     'L0_attn_Wk': 8.0,
     'L0_attn_Wv': 8.0,
     'L0_attn_Wo': 5.123,
     'L0_attn_U': 5.656,
     'L0_attn_V': 7.363,
     'L0_ffn_W1': 3.641,
     'L0_ffn_W2': 3.574,
     'L0_ffn_Wqkv': 4.533,
     'L0_ffn_Wo': 4.73}
    for name, (base, spread) in spreads.items():
        noise = np.random.default_rng([zlib.crc32(name.encode()), seed]).standard_normal(out[name].shape)
        drawn = base * np.exp(spread * noise) if base else spread * noise
        out[name] = jnp.asarray(drawn.astype(out[name].dtype))
    for name, factor in factors.items():
        out[name] = (out[name] * factor).astype(out[name].dtype)
    return out
```

```python
from contextlib import ExitStack

import numpy as np

import concourse.bass as bass
from concourse import mybir

F32 = mybir.dt.float32
BF16 = mybir.dt.bfloat16
ALU = mybir.AluOpType
ACT = mybir.ActivationFunctionType
AX = mybir.AxisListType

P = 128
T = 2048
NT = T // P
CH = 512
NC = T // CH

H = 16
HD = P // H
PARTS = 3
PROD = PARTS * PARTS * HD
MAXROW = 96
VC = 32

DEPTH = 6
DH = 64
INNER = H * DH
WIN = 32
NP = H // 2
FF = int(P * 4 * 2 / 3)
FM = -(-FF // P)
FL = FF - (FM - 1) * P
NEG = -1.0e30


def tables():
    half = np.arange(0, DH, 2, dtype=np.float32)
    inv_freq = (np.float32(1.0) / np.power(np.float32(10000.0), half / np.float32(DH))).astype(np.float32)
    freqs = np.arange(T, dtype=np.float32)[:, None] * inv_freq[None, :]
    freqs = np.concatenate([freqs, freqs], -1).astype(np.float64)
    base = (half.astype(np.float64) + 0.4 * DH) / (1.4 * DH)
    base = np.concatenate([base, base])
    local = (np.arange(T) % P - P // 2) / (WIN // 2)
    scale = base[None, :] ** local[:, None]
    sign = np.where(np.arange(DH) < DH // 2, -1.0, 1.0)[None, :]
    cos, sin = np.cos(freqs), np.sin(freqs) * sign
    lay = lambda a: a.reshape(NT, P, DH).transpose(1, 0, 2)
    rot = np.stack([lay(cos * scale), lay(sin * scale), lay(cos / scale), lay(sin / scale)], 1)
    carry = np.tile(base ** (P / (WIN // 2)), 2)[:, None]
    i, c = np.arange(P)[:, None] % WIN, np.arange(2 * WIN)[None, :]
    ok = (i <= c) & (c <= i + WIN)
    first = ok & ~((np.arange(P)[:, None] < WIN) & (c < WIN))
    mask = np.stack([np.where(first, 0.0, NEG), np.where(ok, 0.0, NEG)], 1)
    ident = np.eye(P)
    f = lambda a: np.ascontiguousarray(a, dtype=np.float32)
    return {"rot": f(rot), "carry": f(carry), "mask": f(mask), "ident": f(ident)}


class Schedule:

    def __init__(self, nc, ctx):
        self.nc, self.ctx = nc, ctx
        self.queues = {"pe": [], "dve": [], "act": [], "pool": [], "sp": []}
        self.counts = {}
        self.sems = {}
        self.pool_last = None

    def sem(self, name):
        if name not in self.sems:
            self.sems[name] = self.ctx.enter_context(self.nc.semaphore(name))
            self.counts[name] = 0
        return name

    def step(self, engine, waits, issue, sem):
        self.sem(sem)
        self.counts[sem] += 1
        mark = (sem, self.counts[sem])
        if engine == "pool":
            waits, self.pool_last = list(waits) + [self.pool_last], mark
        self.queues[engine].append((tuple(waits), issue, sem, 1))
        return mark

    def dma(self, engine, waits, out, in_, sem):
        self.sem(sem)
        self.counts[sem] += 16
        self.queues[engine].append((tuple(waits), lambda e: e.dma_start(out, in_), sem, 16))
        return (sem, self.counts[sem])

    def play(self, engine, e):
        seen = {}
        for waits, issue, sem, inc in self.queues[engine]:
            for mark in waits:
                if mark is not None and seen.get(mark[0], 0) < mark[1]:
                    e.wait_ge(self.sems[mark[0]], mark[1])
                    seen[mark[0]] = mark[1]
            issue(e).then_inc(self.sems[sem], inc)


def rsqrt(s, name, shape, src, tmp, out, lo, ready):
    c, t = tmp
    op = ALU.max if lo[0] == "max" else ALU.add
    a = s.step("dve", ready, lambda e: e.tensor_scalar(c, src, lo[1], None, op), name + "_arg")
    b = s.step("act", [a], lambda e: e.activation(t, c, ACT.Ln), name + "_ln")
    b = s.step("act", [b], lambda e: e.activation(out, t, ACT.Exp, scale=-0.5), name + "_exp")
    d = s.step("dve", [b], lambda e: e.tensor_tensor(t, out, out, ALU.mult), name + "_sq")
    d = s.step("dve", [d], lambda e: e.scalar_tensor_tensor(
        out=t, in0=t, scalar=-0.5, in1=c, op0=ALU.mult, op1=ALU.mult), name + "_sq")
    return s.step("dve", [d], lambda e: e.scalar_tensor_tensor(
        out=out, in0=t, scalar=1.5, in1=out, op0=ALU.add, op1=ALU.mult), name + "_r")


def build(nc, d, out):
    with ExitStack() as ctx:
        s = Schedule(nc, ctx)
        sb = lambda c, n, shape, dt=F32: c.enter_context(nc.sbuf_tensor(n, shape, dt))
        ps = lambda c, n, shape, dt=F32: c.enter_context(nc.psum_tensor(n, shape, dt))

        x_tok = sb(ctx, "x_tok", [P, NT, P])
        att_T = sb(ctx, "att_T", [P, T])
        stream = [sb(ctx, f"stream{i}", [P, T + 1]) for i in range(2)]
        ident = sb(ctx, "ident", [P, P])
        ident_bf = sb(ctx, "ident_bf", [P, P], BF16)
        ones = sb(ctx, "ones", [P, P])
        ones_row = sb(ctx, "ones_row", [1, P])
        carry = sb(ctx, "carry", [P, 1])
        mask_f = sb(ctx, "mask_f", [P, 2, 2 * WIN])
        mask_bf = sb(ctx, "mask_bf", [P, 2, NP, 2 * WIN], BF16)

        m_x = s.dma("sp", [], x_tok[:, :, :], d["x"].rearrange("a (i p) d -> p (a i) d", p=P), "ld_x")
        m_id = s.dma("sp", [], ident[:, :], d["ident"], "ld_id")
        s.dma("sp", [], carry[:, :], d["carry"], "ld_tab")
        m_tab = s.dma("sp", [], mask_f[:, :, :], d["mask"], "ld_tab")

        m_ones = s.step("pool", [], lambda e: e.memset(ones[:, :], 1.0 / P), "const")
        m_ones = s.step("pool", [], lambda e: e.memset(ones_row[:, :], 1.0), "const")
        for i in range(2):
            m_ones = s.step("pool", [], lambda e, i=i: e.memset(stream[i][64:P, 0:1], 0.0), "const")

        with ExitStack() as phase_a:
            done_a = part_a(nc, s, phase_a, sb, ps, d, x_tok, att_T, stream, ident, ident_bf, ones_row,
                            m_x, m_id, m_ones)
        with ExitStack() as phase_b:
            done_b = part_b(nc, s, phase_b, sb, ps, d, stream, ident, ident_bf, ones, ones_row, carry,
                            mask_f, mask_bf, m_tab, m_ones, done_a)

        with ExitStack() as phase_c:
            fin = [ps(phase_c, f"fin{i}", [P, 4, P]) for i in range(2)]
            x0 = stream[0]
            s.step("dve", done_b + done_a, lambda e: e.tensor_tensor(
                att_T[0:64, :], att_T[0:64, :], x0[0:64, 0:T], ALU.add), "fin_sum")
            a = s.step("dve", [], lambda e: e.tensor_tensor(
                att_T[64:P, :], att_T[64:P, :], x0[64:P, 1:T + 1], ALU.add), "fin_sum")
            added = [None, None]
            for g in range(NC):
                def turn(e, g=g):
                    for j in range(4):
                        i = 4 * g + j
                        ins = e.transpose(fin[g % 2][:, j, :], att_T[:, i * P:(i + 1) * P], ident[:, :])
                    return ins
                m = s.step("pe", [a, added[-2]] + done_b, turn, "fin_T")
                tok = x_tok[:, 4 * g:4 * g + 4, :]
                added.append(s.step("dve", [m], lambda e, g=g, tok=tok: e.tensor_tensor(
                    tok, fin[g % 2][:, :, :], tok, ALU.add), "fin_add"))
                m_out = s.dma("sp", [added[-1]], out.rearrange("a (i p) d -> p (a i) d", p=P)[:, 4 * g:4 * g + 4, :],
                              tok, "st_out")
        sems = s.sems
        block = ctx.enter_context(nc.Block())

        @block.sync
        def _(e):
            s.play("sp", e)
            e.wait_ge(sems[m_out[0]], m_out[1])

        @block.gpsimd
        def _(e):
            s.play("pool", e)

        @block.scalar
        def _(e):
            s.play("act", e)

        @block.vector
        def _(e):
            s.play("dve", e)

        @block.tensor
        def _(e):
            s.play("pe", e)


def part_a(nc, s, ctx, sb, ps, d, x_tok, att_T, stream, ident, ident_bf, ones_row, m_x, m_id, m_ones):
    w_raw = {n: sb(ctx, "w_" + n, [P, P]) for n in ("Wq", "Wk", "Wv", "Wo")}
    b_col = {n: sb(ctx, "b_" + n, [P, 1]) for n in ("bq", "bk", "bv", "bo")}
    bdV = sb(ctx, "bdV", [P, P])
    bdU = sb(ctx, "bdU", [P, P])
    xn_T = sb(ctx, "xn_T", [P, T])
    xc = sb(ctx, "xc", [P, NT, P])
    sq = sb(ctx, "sqA", [P, NT, P])
    stat = sb(ctx, "statA", [P, 6, NT])
    w_z = {n: sb(ctx, "wz_" + n, [P, P]) for n in ("Wq", "Wk", "Wv")}
    b_z = {n: sb(ctx, "bz_" + n, [P, 1]) for n in ("bq", "bk")}
    bv_row = sb(ctx, "bv_row", [1, P])
    wo_T = sb(ctx, "wo_T", [P, P])
    w_out = sb(ctx, "w_out", [P, P])
    z = {n: sb(ctx, "z_" + n, [P, T]) for n in "qk"}
    zp = {n: sb(ctx, "zp_" + n, [P, PARTS, T], BF16) for n in "qk"}
    va = sb(ctx, "va", [P, NT, H, VC])
    QS = [sb(ctx, f"QS{i}", [P, T], BF16) for i in range(2)]
    KS = [sb(ctx, f"KS{i}", [P, T], BF16) for i in range(2)]
    mx = [sb(ctx, f"mx{i}", [P, NT, 2]) for i in range(2)]
    nmax = [sb(ctx, f"nmax{i}", [P, NT]) for i in range(2)]
    nm_r = sb(ctx, "nm_r", [NT, P])
    nm_p = [sb(ctx, f"nm_p{i}", [NT, PARTS, P], BF16) for i in range(2)]
    NPT = 8
    PT = [sb(ctx, f"PT{i}", [P, CH]) for i in range(NPT)]
    o_h = [sb(ctx, f"o_h{i}", [P, CH]) for i in range(2)]
    y = z["q"]
    l = z["k"]
    S_ps = [ps(ctx, f"S_ps{i}", [P, 2, CH]) for i in range(2)]
    E_ps = [ps(ctx, f"E_ps{i}", [P, CH]) for i in range(2)]
    O_ps = ps(ctx, "O_ps", [P, CH])
    M_ps = ps(ctx, "M_ps", [P, CH])

    for n in w_raw:
        m_w = s.dma("sp", [], w_raw[n][:, :], d[n], "ld_w")
    for n in b_col:
        m_w = s.dma("sp", [], b_col[n][:, :], d[n].rearrange("(p o) -> p o", o=1), "ld_w")
    m_z = s.step("pool", [], lambda e: e.memset(bdV[:, :], 0.0), "zeroA")
    m_z = s.step("pool", [], lambda e: e.memset(bdU[:, :], 0.0), "zeroA")
    for h in range(H):
        b = slice(h * HD, (h + 1) * HD)
        s.dma("sp" if h % 2 else "act", [m_z], bdV[b, b], d["V"], "ld_bd")
        m_bd = s.dma("act" if h % 2 else "sp", [m_z], bdU[b, b], d["U"], "ld_bd")
    m_va = s.step("pool", [], lambda e: e.memset(va[:, :, :, :], 1.0), "zeroA")
    for i in range(2):
        s.step("pool", [], lambda e, i=i: e.memset(QS[i][64:P, :], 0.0), "zeroA")
        m0 = s.step("pool", [], lambda e, i=i: e.memset(KS[i][64:P, :], 0.0), "zeroA")
        m_st = s.step("pool", [m0], lambda e, i=i: e.memset(KS[i][MAXROW:MAXROW + PARTS, :], 1.0), "zeroA")
    m_idb = s.step("dve", [m_id], lambda e: e.tensor_copy(ident_bf[:, :], ident[:, :]), "idb")

    bc = lambda a: a.unsqueeze(2).to_broadcast([P, NT, P])
    mean, var = stat[:, 0, :], stat[:, 1, :]
    a = s.step("dve", [m_x], lambda e: e.tensor_reduce(mean, x_tok[:, :, :], AX.X, ALU.add), "lnA")
    a = s.step("dve", [a], lambda e: e.tensor_scalar(mean, mean, 1.0 / P, None, ALU.mult), "lnA")
    a = s.step("dve", [a], lambda e: e.tensor_tensor(xc[:, :, :], x_tok[:, :, :], bc(mean), ALU.subtract), "lnA")
    a = s.step("dve", [a], lambda e: e.tensor_tensor(sq[:, :, :], xc[:, :, :], xc[:, :, :], ALU.mult), "lnA")
    a = s.step("dve", [a], lambda e: e.tensor_reduce(var, sq[:, :, :], AX.X, ALU.add), "lnA")
    a = s.step("dve", [a], lambda e: e.tensor_scalar(var, var, 1.0 / P, None, ALU.mult), "lnA")
    r = rsqrt(s, "rA", None, var, (stat[:, 2, :], stat[:, 3, :]), stat[:, 4, :], ("add", 1e-5), [a])
    m_xn = s.step("dve", [r], lambda e: e.tensor_tensor(sq[:, :, :], xc[:, :, :], bc(stat[:, 4, :]), ALU.mult), "lnA")

    scale = 1.0 / float(np.sqrt(np.float32(HD)))
    banks = [S_ps[0][:, 0, :], S_ps[0][:, 1, :], S_ps[1][:, 0, :], S_ps[1][:, 1, :], E_ps[0][:, :], E_ps[1][:, :],
             O_ps[:, :], M_ps[:, :]]
    free = [None] * 8
    turn_n = [0]

    def bank():
        turn_n[0] = (turn_n[0] + 1) % 8
        return turn_n[0]

    def small(waits, mm, evac, sem):
        b = bank()
        m = s.step("pe", waits + [free[b]], lambda e: mm(e, banks[b]), sem + "_mm")
        free[b] = s.step("dve", [m], lambda e: evac(e, banks[b]), sem)
        return free[b]

    for n in ("Wq", "Wk", "Wv"):
        k = scale if n == "Wq" else 1.0
        m_wz = small([m_w, m_bd], lambda e, b, n=n: e.matmul(b[:, 0:P], w_raw[n][:, :], bdV[:, :], start=True, stop=True),
                     lambda e, b, n=n, k=k: e.tensor_scalar(w_z[n][:, :], b[:, 0:P], k, None, ALU.mult), "fold")
    for n in ("bq", "bk"):
        k = scale if n == "bq" else 1.0
        m_wz = small([], lambda e, b, n=n: e.matmul(b[:, 0:1], bdV[:, :], b_col[n][:, :], start=True, stop=True),
                     lambda e, b, n=n, k=k: e.tensor_scalar(b_z[n][:, :], b[:, 0:1], k, None, ALU.mult), "fold")
    m_wz = small([], lambda e, b: e.matmul(b[0:1, 0:P], b_col["bv"][:, :], bdV[:, :], start=True, stop=True),
                 lambda e, b: e.tensor_copy(bv_row[:, :], b[0:1, 0:P]), "fold")
    m_wt = small([m_id], lambda e, b: e.transpose(b[:, 0:P], w_raw["Wo"][:, :], ident[:, :]),
                 lambda e, b: e.tensor_copy(wo_T[:, :], b[:, 0:P]), "fold")
    m_wz = small([m_wt], lambda e, b: e.matmul(b[:, 0:P], bdU[:, :], wo_T[:, :], start=True, stop=True),
                 lambda e, b: e.tensor_copy(w_out[:, :], b[:, 0:P]), "fold")

    for g in range(NC):
        def turn(e, bk, g=g):
            for j in range(4):
                ins = e.transpose(bk[:, j * P:(j + 1) * P], sq[:, 4 * g + j, :], ident[:, :])
            return ins
        b = bank()
        m = s.step("pe", [m_xn, m_id, free[b]], lambda e, b=b, t=turn: t(e, banks[b]), "xT_mm")
        c = slice(g * CH, (g + 1) * CH)
        free[b] = s.step("act", [m], lambda e, b=b, c=c: e.activation(xn_T[:, c], banks[b], ACT.Copy), "xT")
        s.step("pool", [free[b]], lambda e, c=c: e.tensor_copy(stream[0][0:64, c], xn_T[0:64, c]), "skew")
        m_skew = s.step("pool", [], lambda e, c=c, g=g: e.tensor_copy(
            stream[0][64:P, g * CH + 1:(g + 1) * CH + 1], xn_T[64:P, c]), "skew")
        m_xT = free[b]

    m_part = {}
    for n, w, bz in (("q", "Wq", "bq"), ("k", "Wk", "bk")):
        for g in range(NC):
            c = slice(g * CH, (g + 1) * CH)
            b = bank()
            m = s.step("pe", [m_xT, m_wz, free[b]], lambda e, b=b, c=c, w=w: e.matmul(
                banks[b], w_z[w][:, :], xn_T[:, c], start=True, stop=True), "z_mm")
            free[b] = s.step("act", [m], lambda e, b=b, c=c, n=n, bz=bz: e.activation(
                z[n][:, c], banks[b], ACT.Identity, bias=b_z[bz][:, 0:1]), "z")
        a = free[b]
        for i in range(PARTS):
            a = s.step("dve", [a], lambda e, n=n, i=i: e.tensor_copy(zp[n][:, i, :], z[n][:, :]), "part")
            if i < PARTS - 1:
                a = s.step("dve", [a], lambda e, n=n, i=i: e.tensor_tensor(
                    z[n][:, :], z[n][:, :], zp[n][:, i, :], ALU.subtract), "part")
        m_part[n] = a

    for g in range(NC):
        def vals(e, bk, g=g):
            for j in range(4):
                i = 4 * g + j
                e.matmul(bk[:, j * P:(j + 1) * P], xn_T[:, i * P:(i + 1) * P], w_z["Wv"][:, :],
                         start=(j == 0), stop=False, skip_group_check=True)
                ins = e.matmul(bk[:, j * P:(j + 1) * P], ones_row[:, :], bv_row[:, :],
                               start=False, stop=True, skip_group_check=True)
            return ins
        b = bank()
        m = s.step("pe", [free[b], m_ones], lambda e, b=b, f=vals: f(e, banks[b]), "v_mm")
        free[b] = s.step("act", [m, m_va], lambda e, b=b, g=g: e.activation(
            va[:, 4 * g:4 * g + 4, :, 0:HD],
            banks[b].rearrange("p (j h d) -> p j h d", j=4, h=H), ACT.Copy), "va")
        m_vals = free[b]

    m_stack = {}
    m_pass1 = {}
    m_pass2 = {}
    reads = []
    exps = []
    pvs = []
    m_nrow = {}
    m_oev = {}
    m_tr = {}
    m_nmdma = {}
    m_odma = {}

    def stack(h):
        sl = h % 2
        w = [m_part["q"], m_part["k"], m_st] + ([m_pass2[h - 2]] if h >= 2 else [])
        rows = slice(h * HD, (h + 1) * HD)
        for i in range(PARTS):
            for j in range(PARTS):
                to = slice((PARTS * i + j) * HD, (PARTS * i + j + 1) * HD)
                s.dma("sp", w, QS[sl][to, :], zp["q"][rows, i, :], f"ld_stack{sl}")
                m_stack[h] = s.dma("sp", w, KS[sl][to, :], zp["k"][rows, j, :], f"ld_stack{sl}")

    def scores(h, i):
        sl = h % 2
        for hf in range(2):
            n = len(reads)
            def mm(e, sl=sl, i=i, hf=hf, n=n):
                for c in range(2):
                    k = (2 * hf + c) * CH
                    ins = e.matmul(S_ps[n % 2][:, c, :], QS[sl][0:MAXROW, i * P:(i + 1) * P],
                                   KS[sl][0:MAXROW, k:k + CH], start=True, stop=True)
                return ins
            m = s.step("pe", [m_stack[h], reads[n - 2] if n >= 2 else free_all], mm, "sc_mm")
            reads.append(s.step("dve", [m, m_tr.get(h - 2)], lambda e, h=h, i=i, hf=hf, n=n: e.tensor_reduce(
                mx[h % 2][:, i, hf:hf + 1], S_ps[n % 2][:, :, :], AX.XY, ALU.max), "sc_max"))
        m_pass1[h] = m

    def max_rows(h):
        sl = h % 2
        a = s.step("dve", [reads[-1]], lambda e: e.tensor_reduce(nmax[sl][:, :], mx[sl][:, :, :], AX.X, ALU.max, negate=True), "nm")
        m_tr[h] = a
        a = s.step("pe", [a, m_nrow.get(h - 1), m_id], lambda e: e.transpose(M_ps[0:NT, 0:P], nmax[sl][:, :], ident[:, :]), "nm_T")
        a = s.step("dve", [a], lambda e: e.tensor_copy(nm_r[:, :], M_ps[0:NT, 0:P]), "nm")
        m_nrow[h] = a
        for i in range(PARTS):
            a = s.step("dve", [a, m_nmdma.get(h - 2)], lambda e, i=i: e.tensor_copy(nm_p[sl][:, i, :], nm_r[:, :]), "nm")
            if i < PARTS - 1:
                a = s.step("dve", [a], lambda e, i=i: e.tensor_tensor(nm_r[:, :], nm_r[:, :], nm_p[sl][:, i, :], ALU.subtract), "nm")
        for i in range(PARTS):
            m_nmdma[h] = s.dma("sp", [a, m_pass2.get(h - 2)], QS[sl][MAXROW + i:MAXROW + i + 1, :], nm_p[sl][:, i, :], f"ld_max{sl}")

    def probs(h, j):
        sl = h % 2
        for c in range(NC):
            n = len(exps)
            m = s.step("pe", [m_nmdma[h], exps[n - 2] if n >= 2 else free_all], lambda e, sl=sl, j=j, c=c, n=n: e.matmul(
                E_ps[n % 2][:, :], KS[sl][0:MAXROW + PARTS, j * P:(j + 1) * P],
                QS[sl][0:MAXROW + PARTS, c * CH:(c + 1) * CH], start=True, stop=True), "pr_mm")
            exps.append(s.step("act", [m, pvs[n - NPT] if n >= NPT else None], lambda e, n=n: e.activation(
                PT[n % NPT][:, :], E_ps[n % 2][:, :], ACT.Exp), "pr_exp"))
        m_pass2[h] = m

    def values(h, j):
        for c in range(NC):
            n = len(pvs)
            pvs.append(s.step("pe", [exps[n], m_vals, m_oev.get(h - 1)] if j == 0 else [exps[n]],
                              lambda e, h=h, j=j, c=c, n=n: e.matmul(
                O_ps[VC * c:VC * (c + 1), :], va[:, j, h, :], PT[n % NPT][:, :], start=(j == 0), stop=(j == NT - 1)), "pv"))
        if j == NT - 1:
            sl = h % 2
            m_oev[h] = s.step("dve", [pvs[-1], m_odma.get(h - 2)], lambda e: e.tensor_copy(o_h[sl][:, :], O_ps[:, :]), "o_ev")
            rows = slice(h * HD, (h + 1) * HD)
            for c in range(NC):
                s.dma("sp", [m_oev[h], m_part["q"]], y[rows, c * CH:(c + 1) * CH], o_h[sl][VC * c:VC * c + HD, :], f"ld_o{sl}")
                m_odma[h] = s.dma("sp", [m_oev[h], m_part["k"]], l[rows, c * CH:(c + 1) * CH], o_h[sl][VC * c + HD:VC * c + 2 * HD, :], f"ld_o{sl}")

    free_all = s.step("pe", free, lambda e: e.matmul(M_ps[0:1, 0:1], ones_row[0:1, 0:1], ones_row[0:1, 0:1], start=True, stop=True), "prep")
    stack(0)
    for i in range(NT):
        scores(0, i)
    stack(1)
    max_rows(0)
    for h in range(H):
        if 1 <= h < H - 1:
            stack(h + 1)
        for j in range(NT):
            if h + 1 < H:
                scores(h + 1, j)
            probs(h, j)
            if j:
                values(h, j - 1)
        if h + 1 < H:
            max_rows(h + 1)
        values(h, NT - 1)

    a = s.step("dve", [m_odma[H - 1], m_odma[H - 2]], lambda e: e.reciprocal(l[:, :], l[:, :]), "norm")
    a = s.step("dve", [a], lambda e: e.tensor_tensor(y[:, :], y[:, :], l[:, :], ALU.mult), "norm")
    for g in range(NC):
        c = slice(g * CH, (g + 1) * CH)
        bk = banks[g]
        m = s.step("pe", [a, reads[-1], reads[-2], exps[-1], exps[-2]], lambda e, bk=bk, c=c: e.matmul(bk, w_out[:, :], y[:, c], start=True, stop=True), "att_mm")
        m_att = s.step("act", [m], lambda e, bk=bk, c=c: e.activation(att_T[:, c], bk, ACT.Identity, bias=b_col["bo"][:, 0:1]), "att")
    return [m_att, m_skew, pvs[-1], m_oev[H - 1], m_odma[H - 1], m_odma[H - 2], m_part["k"], m_idb]


def part_b(nc, s, ctx, sb, ps, d, stream, ident, ident_bf, ones, ones_row, carry, mask_f, mask_bf, m_tab, m_ones, done_a):
    w_qkv = sb(ctx, "w_qkv", [P, 3 * INNER])
    w_o = sb(ctx, "w_o", [P, NP, P])
    w_1 = sb(ctx, "w_1", [P, 2 * FF])
    w_2 = sb(ctx, "w_2", [P, FM, P])
    b_1 = sb(ctx, "b_1", [P, 2, FM])
    cols = sb(ctx, "cols", [P, 3])
    rot = sb(ctx, "rot", [P, 4, NT, DH])
    gains = sb(ctx, "gains", [P, 2, DH])
    sq = sb(ctx, "sq", [P, INNER])
    ss = [sb(ctx, f"ss{i}", [P, 2 * H]) for i in range(2)]
    rs = [[sb(ctx, f"rs{i}{j}", [P, 2 * H]) for j in range(3)] for i in range(2)]
    nrm = [sb(ctx, f"nrm{i}", [P, INNER]) for i in range(2)]
    tc = [sb(ctx, f"tc{i}", [P, INNER]) for i in range(2)]
    ts = [sb(ctx, f"ts{i}", [P, INNER]) for i in range(2)]
    q_T = sb(ctx, "q_T", [P, NP, P])
    k_T = [sb(ctx, f"k_T{i}", [P, NP, WIN + P]) for i in range(2)]
    v = [sb(ctx, f"v{i}", [P, INNER]) for i in range(3)]
    v_sh = [sb(ctx, f"v_sh{i}", [P, INNER]) for i in range(2)]
    pr = [sb(ctx, f"pr{i}", [P, H, 2 * WIN]) for i in range(2)]
    mx = sb(ctx, "mxB", [P, 3, H])
    pT = [sb(ctx, f"pT{i}", [P, H, P]) for i in range(2)]
    o_T = [sb(ctx, f"o_T{i}", [P, NP, P]) for i in range(2)]
    xl = sb(ctx, "xl", [P, T])
    lnb = sb(ctx, "lnb", [P, CH])
    row = sb(ctx, "row", [1, 4, CH])
    hid = sb(ctx, "hid", [P, FM, CH])
    gel = [sb(ctx, f"gel{i}", [P, CH]) for i in range(2)]
    W_ps = [ps(ctx, f"W_ps{i}", [P, 2, CH]) for i in range(2)]
    T_ps = [ps(ctx, f"T_ps{i}", [P, 4, P]) for i in range(2)]
    S_ps = ps(ctx, "SB_ps", [P, 2, NP, 2 * WIN])

    m_mask = s.step("dve", [m_tab] + done_a, lambda e: e.tensor_copy(
        mask_bf[:, :, :, :], mask_f[:, :, :].unsqueeze(2).to_broadcast([P, 2, NP, 2 * WIN])), "mask")
    for i in range(2):
        s.step("pool", done_a, lambda e, i=i: e.memset(pT[i][:, :, :], 0.0), "zeroB")
        s.step("pool", [], lambda e, i=i: e.memset(v_sh[i][0:WIN, :], 0.0), "zeroB")
        m_zero = s.step("pool", [], lambda e, i=i: e.memset(k_T[i][:, :, 0:WIN], 0.0), "zeroB")

    last = {}

    def L(*names):
        return [last.get(n) for n in names]

    t_uses = []
    x_in, x_out = stream
    x_ready = [done_a] * NC
    w_uses = []

    def load_attn(n):
        w = done_a + L("proj_mm", "y_mm")
        for j in range(3):
            c = slice(j * INNER, (j + 1) * INNER)
            last["w_qkv"] = s.dma("sp", w, w_qkv[:, c], d["Wqkv"][n][:, c], "ld_wqkv")
        last["w_o"] = s.dma("sp", w, w_o[:, :, :], d["Wo2"][n].rearrange("(k p) n -> p k n", p=P), "ld_wo")
        w = done_a + L("rot_use_d", "rot_use_p")
        s.dma("sp", w, rot[:, :, :, :], d["rot"], "ld_rot")
        s.dma("sp", w, gains[:, 0, :], d["q_scale"][n:n + 1, :].to_broadcast([P, DH]), "ld_rot")
        m = s.dma("sp", w, gains[:, 1, :], d["k_scale"][n:n + 1, :].to_broadcast([P, DH]), "ld_rot")
        HF = DH // 2
        for i in range(2):
            g = gains[:, i, :]
            b = lambda a, k: a.unsqueeze(1).to_broadcast([P, NT, k])
            s.step("pool", [m], lambda e, i=i, g=g: e.tensor_tensor(rot[:, 2 * i, :, :], rot[:, 2 * i, :, :], b(g, DH), ALU.mult), "rot")
            s.step("pool", [m], lambda e, i=i, g=g: e.tensor_tensor(
                rot[:, 2 * i + 1, :, 0:HF], rot[:, 2 * i + 1, :, 0:HF], b(g[:, HF:DH], HF), ALU.mult), "rot")
            last["rot"] = s.step("pool", [m], lambda e, i=i, g=g: e.tensor_tensor(
                rot[:, 2 * i + 1, :, HF:DH], rot[:, 2 * i + 1, :, HF:DH], b(g[:, 0:HF], HF), ALU.mult), "rot")

    def load_mlp(n):
        w = done_a + L("up_mm", "down_mm", "ffn_dve", "gelu")
        s.dma("sp", w, w_1[:, :], d["W1"][n], "ld_mlp")
        s.dma("sp", w, w_2[:, 0:FM - 1, :], d["W2"][n][0:(FM - 1) * P, :].rearrange("(k p) n -> p k n", p=P), "ld_mlp")
        s.dma("sp", w, w_2[0:FL, FM - 1, :], d["W2"][n][(FM - 1) * P:FF, :], "ld_mlp")
        for i in range(2):
            o = i * FF
            b = d["b1"][n]
            for k in range(FM):
                m = P if k < FM - 1 else FL
                s.dma("sp", w, b_1[0:m, i, k:k + 1], b[o + k * P:o + k * P + m].rearrange("(p o) -> p o", o=1), "ld_mlp")
        for i, nme in enumerate(("ln_g", "ln_b", "b2")):
            last["mlp_w"] = s.dma("sp", w, cols[:, i:i + 1], d[nme][n].rearrange("(p o) -> p o", o=1), "ld_mlp")

    def project(tile, which):
        n = len(w_uses)
        c = tile * P // CH
        def mm(e, tile=tile, which=which, n=n):
            for hf in range(2):
                o = which * INNER + hf * CH
                ins = e.matmul(W_ps[n % 2][:, hf, :], x_in[:, tile * P:(tile + 1) * P], w_qkv[:, o:o + CH],
                               start=True, stop=True)
            return ins
        m = s.step("pe", list(x_ready[c]) + L("w_qkv") + [w_uses[n - 2] if n >= 2 else None], mm, "proj")
        last["proj_mm"] = m
        w_uses.append(None)
        return n, m

    def norms(tile, pn):
        st = tile % 2
        for i, (n, m) in enumerate(pn):
            a = s.step("act", [m, last.get("ss_red")], lambda e, n=n: e.activation(
                sq[:, :].rearrange("p (a b) -> p a b", a=2), W_ps[n % 2][:, :, :], ACT.Square), "sq")
            last["ss_red"] = s.step("dve", [a, last.get(("rs", st))], lambda e, i=i, st=st: e.tensor_reduce(
                ss[st][:, i * H:(i + 1) * H], sq[:, :].rearrange("p (h d) -> p h d", h=H), AX.X, ALU.add), "ss")
        r = rs[st]
        m_r = rsqrt(s, "rB", None, ss[st][:, :], (r[0][:, :], r[1][:, :]), r[2][:, :], ("max", 1e-24), [last["ss_red"]])
        last[("rs", st)] = m_r
        return m_r

    def rotate(tile, pn, m_r):
        st = tile % 2
        HF = DH // 2
        marks = []
        for i, (n, m) in enumerate(pn):
            view = lambda a: a.rearrange("p (h d) -> p h d", h=H)
            a = s.step("dve", [m_r, last.get(("nrm", i))], lambda e, i=i, n=n: e.tensor_tensor(
                view(nrm[i][:, :]), W_ps[n % 2][:, :, :].rearrange("p a (h d) -> p (a h) d", d=DH),
                rs[st][2][:, i * H:(i + 1) * H].unsqueeze(2).to_broadcast([P, H, DH]), ALU.mult), "nrm")
            w_uses[n] = a
            eng = "dve" if i == 0 else "pool"
            cosn, sinn = rot[:, 2 * i, tile, :], rot[:, 2 * i + 1, tile, :]
            b = lambda t, k: t.unsqueeze(1).to_broadcast([P, H, k])
            s.step(eng, [a, last.get("rot"), last.get(("tc", i))], lambda e, i=i, c=cosn: e.tensor_tensor(
                view(tc[i][:, :]), view(nrm[i][:, :]), b(c, DH), ALU.mult), f"trig{i}")
            s.step(eng, [a, last.get(("ts", i))], lambda e, i=i, c=sinn: e.tensor_tensor(
                view(ts[i][:, :])[:, :, 0:HF], view(nrm[i][:, :])[:, :, HF:DH], b(c[:, 0:HF], HF), ALU.mult), f"trig{i}")
            a = s.step(eng, [a], lambda e, i=i, c=sinn: e.tensor_tensor(
                view(ts[i][:, :])[:, :, HF:DH], view(nrm[i][:, :])[:, :, 0:HF], b(c[:, HF:DH], HF), ALU.mult), f"trig{i}")
            last[("nrm", i)] = a
            last["rot_use_d" if i == 0 else "rot_use_p"] = a
            a = s.step("pool", [a], lambda e, i=i: e.tensor_tensor(tc[i][:, :], tc[i][:, :], ts[i][:, :], ALU.add), "rotsum")
            last[("ts", i)] = a
            marks.append(a)
        return marks

    def turn(tile, rotated):
        for i in range(2):
            for hf in range(2):
                n = len(t_uses)
                def tr(e, i=i, hf=hf, n=n):
                    for j in range(4):
                        b = 4 * hf + j
                        ins = e.transpose(T_ps[n % 2][:, j, :], tc[i][:, b * P:(b + 1) * P], ident[:, :])
                    return ins
                m = s.step("pe", [rotated[i], t_uses[n - 2] if n >= 2 else None], tr, "turn_mm")
                pslot = slice(4 * hf, 4 * hf + 4)
                if i == 0:
                    a = s.step("act", [m, last.get("score")], lambda e, n=n, pslot=pslot: e.activation(
                        q_T[:, pslot, :], T_ps[n % 2][:, :, :], ACT.Copy), "turn")
                else:
                    kt, kn = k_T[tile % 2], k_T[(tile + 1) % 2]
                    s.step("act", [m, last.get(("k", tile % 2)), m_zero], lambda e, n=n, pslot=pslot, kt=kt: e.activation(
                        kt[:, pslot, WIN:WIN + P], T_ps[n % 2][:, :, :], ACT.Copy), "turn")
                    a = s.step("act", [last.get(("k", (tile + 1) % 2))], lambda e, n=n, pslot=pslot, kn=kn: e.activation(
                        kn[:, pslot, 0:WIN], T_ps[n % 2][:, :, P - WIN:P], ACT.Copy, scale=carry[:, 0:1]), "turn")
                t_uses.append(a)
            last[("tc", i)] = m
        return a

    v_marks = {}

    def keep_v(tile, n, m):
        sl, sh = v[tile % 3], v_sh[tile % 2]
        a = s.step("act", [m, v_marks.get(("use", tile - 3)), v_marks.get(("sh", tile - 3)), v_marks.get(("sh", tile - 2))],
                   lambda e, n=n, sl=sl: e.activation(
            sl[:, :].rearrange("p (a b) -> p a b", a=2), W_ps[n % 2][:, :, :], ACT.Copy), "v")
        w_uses[n] = a
        v_marks[("v", tile)] = a
        w = [a, v_marks.get(("use", tile - 2)), m_zero]
        key = f"ld_vsh{tile % 2}"
        b = s.dma("sp", w, sh[WIN:P, :], sl[0:P - WIN, :], key)
        if tile:
            b = s.dma("sp", w + [v_marks[("v", tile - 1)]], sh[0:WIN, :], v[(tile - 1) % 3][P - WIN:P, :], key)
        v_marks[("sh", tile)] = b

    def score(tile, m_kq):
        kt = k_T[tile % 2]
        mk = mask_bf[:, 0 if tile == 0 else 1, :, :]
        def mm(e, kt=kt, mk=mk):
            for par in range(2):
                e.matmul(S_ps[:, par, :, :], ident_bf[:, :], mk, start=True, stop=False, skip_group_check=True)
            for p in range(NP):
                for par in range(2):
                    r = slice(DH * par, DH * (par + 1))
                    for w in range(P // WIN):
                        ins = e.matmul(S_ps[WIN * w:WIN * (w + 1), par, p, :], q_T[r, p, WIN * w:WIN * (w + 1)],
                                       kt[r, p, WIN * w:WIN * w + 2 * WIN], start=False, stop=True, skip_group_check=True)
            return ins
        m = s.step("pe", [m_kq, m_mask, last.get("s_read")], mm, "score_mm")
        last["score"] = m
        last[("k", tile % 2)] = m
        pb = pr[tile % 2]
        sv = S_ps[:, :, :, :].rearrange("p a b c -> p (a b) c")
        bc = lambda a: a.unsqueeze(2).to_broadcast([P, H, 2 * WIN])
        a = s.step("dve", [m], lambda e: e.tensor_reduce(mx[:, 0, :], sv, AX.X, ALU.max), "sm")
        a = s.step("dve", [a, last.get(("pr", tile % 2))], lambda e: e.tensor_tensor(pb[:, :, :], sv, bc(mx[:, 0, :]), ALU.subtract), "sm")
        last["s_read"] = a
        a = s.step("act", [a], lambda e: e.activation(pb[:, :, :], pb[:, :, :], ACT.Exp, scale=8.0), "smexp")
        a = s.step("dve", [a, last.get("p_norm")], lambda e: e.tensor_reduce(mx[:, 1, :], pb[:, :, :], AX.X, ALU.add), "sm")
        a = s.step("dve", [a], lambda e: e.reciprocal(mx[:, 2, :], mx[:, 1, :]), "sm")
        a = s.step("pool", [a], lambda e: e.tensor_tensor(pb[:, :, :], pb[:, :, :], bc(mx[:, 2, :]), ALU.mult), "pnorm")
        last["p_norm"] = a
        for w in range(P // WIN):
            r = slice(WIN * w, WIN * (w + 1))
            for i in range(2):
                a2 = s.step("dve", [a, last.get("pv"), m_zero], lambda e, r=r, i=i: e.transpose(
                    pT[i][r, :, r.start:r.stop], pb[r, :, WIN * i:WIN * (i + 1)]), "pT")
        last[("pr", tile % 2)] = a2
        return a2

    def values(tile, m_p):
        ot = o_T[tile % 2]
        for hf in range(2):
            n = len(t_uses)
            def mm(e, hf=hf, n=n, tile=tile):
                for j in range(4):
                    p = 4 * hf + j
                    for i in range(2):
                        vv = (v_sh[tile % 2], v[tile % 3])[i]
                        for par in range(2):
                            f = (2 * p + par) * DH
                            ins = e.matmul(T_ps[n % 2][DH * par:DH * (par + 1), j, :], vv[:, f:f + DH],
                                           pT[i][:, par * NP + p, :], start=(j == 0 and i == 0), stop=(i == 1), skip_group_check=True)
                return ins
            m = s.step("pe", [m_p, v_marks[("sh", tile)], v_marks[("v", tile)], t_uses[n - 2]], mm, "pv_mm")
            a = s.step("act", [m, last.get(("o", tile % 2))], lambda e, n=n, hf=hf: e.activation(
                ot[:, 4 * hf:4 * hf + 4, :], T_ps[n % 2][:, :, :], ACT.Copy), "o_T")
            t_uses.append(a)
        last["pv"] = m
        v_marks[("use", tile)] = m
        n = len(t_uses)
        def out(e, n=n):
            for p in range(NP):
                ins = e.matmul(T_ps[n % 2][:, 0, :], w_o[:, p, :], ot[:, p, :], start=(p == 0), stop=(p == NP - 1))
            return ins
        m = s.step("pe", [a, last["w_o"], t_uses[n - 2]], out, "y_mm")
        last["y_mm"] = m
        last[("o", tile % 2)] = m
        c0 = tile * P
        s.step("dve", [m] + list(x_ready[c0 // CH]), lambda e, n=n: e.tensor_tensor(
            x_out[0:64, c0:c0 + P], T_ps[n % 2][0:64, 0, :], x_in[0:64, c0:c0 + P], ALU.add), "resid")
        a = s.step("dve", [], lambda e, n=n: e.tensor_tensor(
            x_out[64:P, c0 + 1:c0 + P + 1], T_ps[n % 2][64:P, 0, :], x_in[64:P, c0 + 1:c0 + P + 1], ALU.add), "resid")
        t_uses.append(a)
        return a

    def mlp(m_res):
        SB = S_ps[:, :, :, :].rearrange("p a b c -> p a (b c)")
        xl_ready, r_marks = [], []
        for g in range(NC):
            c = slice(g * CH, (g + 1) * CH)
            n = len(t_uses)
            tp = T_ps[n % 2][:, :, :].rearrange("p a b -> p (a b)")
            m = s.step("pe", [m_res, t_uses[n - 2]], lambda e, c=c, tp=tp: e.matmul(tp, ones[:, :], x_out[:, c], start=True, stop=True), "mean_mm")
            a = s.step("dve", [m, last.get("xl")], lambda e, c=c, tp=tp: e.tensor_tensor(xl[:, c], x_out[:, c], tp, ALU.subtract), "xc")
            t_uses.append(a)
            q = s.step("act", [a, last.get("var_mm")], lambda e, c=c: e.activation(lnb[:, :], xl[:, c], ACT.Square), "lnsq")
            n = len(t_uses)
            tv = T_ps[n % 2][0:1, :, :].rearrange("p a b -> p (a b)")
            m = s.step("pe", [q, t_uses[n - 2]], lambda e, tv=tv: e.matmul(tv, ones[:, 0:1], lnb[:, :], start=True, stop=True), "var_mm")
            last["var_mm"] = m
            r = rsqrt(s, "rL", None, tv, (row[:, 0, :], row[:, 1, :]), row[:, 2, :], ("add", 1e-5), [m, last.get("bc_mm")])
            t_uses.append(r)
            n = len(t_uses)
            tb = T_ps[n % 2][:, :, :].rearrange("p a b -> p (a b)")
            m = s.step("pe", [r, t_uses[n - 2]], lambda e, tb=tb: e.matmul(tb, ones_row[:, :], row[:, 2, :], start=True, stop=True), "bc_mm")
            last["bc_mm"] = m
            a = s.step("dve", [m], lambda e, c=c, tb=tb: e.tensor_tensor(xl[:, c], xl[:, c], tb, ALU.mult), "xc")
            t_uses.append(a)
            a = s.step("dve", [a, last["mlp_w"]], lambda e, c=c: e.tensor_scalar(
                xl[:, c], xl[:, c], cols[:, 0:1], cols[:, 1:2], ALU.mult, ALU.add), "xc")
            xl_ready.append(a)
        banks = [W_ps[0][:, 0, :], W_ps[0][:, 1, :], W_ps[1][:, 0, :], W_ps[1][:, 1, :]]
        bk_free = [w_uses[-1], w_uses[-1], w_uses[-1], w_uses[-1]]
        bk_free = [[w_uses[-1], w_uses[-2]] for _ in range(4)]
        new = []
        k_n = 0
        for g in range(NC):
            c = slice(g * CH, (g + 1) * CH)
            for k in range(FM):
                w = P if k < FM - 1 else FL
                gb, ab = banks[k_n % 4], banks[(k_n + 1) % 4]
                fg, fa = bk_free[k_n % 4], bk_free[(k_n + 1) % 4]
                m1 = s.step("pe", [xl_ready[g], last["mlp_w"]] + fg, lambda e, k=k, w=w, gb=gb, c=c: e.matmul(
                    gb[0:w, :], w_1[:, FF + k * P:FF + k * P + w], xl[:, c], start=True, stop=True), "up")
                m2 = s.step("pe", fa, lambda e, k=k, w=w, ab=ab, c=c: e.matmul(
                    ab[0:w, :], w_1[:, k * P:k * P + w], xl[:, c], start=True, stop=True), "up")
                gl = gel[k_n // 2 % 2]
                a1 = s.step("act", [m1, last.get(("gel", k_n // 2 % 2))], lambda e, k=k, w=w, gb=gb, gl=gl: e.activation(
                    gl[0:w, :], gb[0:w, :], ACT.Gelu, bias=b_1[0:w, 1, k:k + 1]), "gelu")
                a2 = s.step("dve", [a1, m2, last.get("down_mm")], lambda e, k=k, w=w, ab=ab, gl=gl: e.scalar_tensor_tensor(
                    out=hid[0:w, k, :], in0=ab[0:w, :], scalar=b_1[0:w, 0, k:k + 1], in1=gl[0:w, :],
                    op0=ALU.add, op1=ALU.mult), "hid")
                last[("gel", k_n // 2 % 2)] = a2
                bk_free[k_n % 4], bk_free[(k_n + 1) % 4] = [a1], [a2]
                k_n += 2
            last["up_mm"], last["gelu"], last["xl"] = m2, a1, m2
            yb = SB[:, g % 2, :]
            def down(e, yb=yb):
                for k in range(FM):
                    w = P if k < FM - 1 else FL
                    ins = e.matmul(yb, w_2[0:w, k, :], hid[0:w, k, :], start=(k == 0), stop=(k == FM - 1))
                return ins
            m = s.step("pe", [a2, last.get("s_read"), last.get(("y", g % 2))], down, "down")
            last["down_mm"] = m
            s.step("dve", [m], lambda e, c=c, yb=yb: e.scalar_tensor_tensor(
                out=x_in[0:64, c], in0=yb[0:64, :], scalar=cols[0:64, 2:3], in1=x_out[0:64, c], op0=ALU.add, op1=ALU.add), "resid2")
            o = slice(g * CH + 1, (g + 1) * CH + 1)
            a = s.step("dve", [], lambda e, o=o, yb=yb: e.scalar_tensor_tensor(
                out=x_in[64:P, o], in0=yb[64:P, :], scalar=cols[64:P, 2:3], in1=x_out[64:P, o], op0=ALU.add, op1=ALU.add), "resid2")
            last[("y", g % 2)] = a
            new.append([a])
        last["ffn_dve"] = a
        last["s_read"] = a
        w_uses.extend([bk_free[1][0], bk_free[3][0]] if len(w_uses) % 2 == 0 else [bk_free[3][0], bk_free[1][0]])
        return new

    load_attn(0)
    load_mlp(0)
    for layer in range(DEPTH):
        kept, m_p, m_res = {}, {}, None
        for i in range(NT + 2):
            if i < NT:
                q, k = project(i, 0), project(i, 1)
                m_r = norms(i, (q, k))
            if 1 <= i <= NT:
                m_kq = turn(i - 1, kept["rot"])
            if i >= 2:
                m_res = values(i - 2, m_p[i - 2])
            if i < NT:
                rotated = rotate(i, (q, k), m_r)
            if 1 <= i <= NT:
                m_p[i - 1] = score(i - 1, m_kq)
            if i < NT:
                n, m = project(i, 2)
                keep_v(i, n, m)
                kept["rot"] = rotated
        if layer + 1 < DEPTH:
            load_attn(layer + 1)
        x_ready = mlp(m_res)
        if layer + 1 < DEPTH:
            load_mlp(layer + 1)
    return [x_ready[-1][0], t_uses[-1], t_uses[-2]]


_INS = {"L0_attn_x": "x", "L0_attn_Wq": "Wq", "L0_attn_bq": "bq", "L0_attn_Wk": "Wk", "L0_attn_bk": "bk",
        "L0_attn_Wv": "Wv", "L0_attn_bv": "bv", "L0_attn_Wo": "Wo", "L0_attn_bo": "bo", "L0_attn_U": "U",
        "L0_attn_V": "V", "L0_ffn_Wqkv": "Wqkv", "L0_ffn_q_scale": "q_scale", "L0_ffn_k_scale": "k_scale",
        "L0_ffn_Wo": "Wo2", "L0_ffn_ln_g": "ln_g", "L0_ffn_ln_b": "ln_b", "L0_ffn_W1": "W1", "L0_ffn_b1": "b1",
        "L0_ffn_W2": "W2", "L0_ffn_b2": "b2"}


def kernel(**inputs):
    import concourse.bacc as _bacc
    from concourse.bass_utils import run_bass_kernel_spmd as _run

    nc = _bacc.Bacc("TRN2", target_bir_lowering=False, num_devices=1)
    arrays, args = {}, {}
    for name, short in _INS.items():
        arrays[f"in_{short}"] = np.ascontiguousarray(inputs[name])
    for name, a in tables().items():
        arrays[f"in_{name}"] = a
    for name, a in arrays.items():
        args[name[3:]] = nc.dram_tensor(name, a.shape, mybir.dt.from_np(a.dtype), kind="ExternalInput").ap()
    out = nc.dram_tensor("out", (1, T, P), F32, kind="ExternalOutput").ap()
    build(nc, args, out)
    return _run(nc, [arrays], core_ids=[0]).results[0]["out"]
```

```python
from contextlib import ExitStack

import numpy as np

import concourse.bass as bass
from concourse import mybir

F32 = mybir.dt.float32
BF16 = mybir.dt.bfloat16
ALU = mybir.AluOpType
ACT = mybir.ActivationFunctionType
AX = mybir.AxisListType

P = 128
T = 2048
NT = T // P
CH = 512
NC = T // CH

H = 16
HD = P // H
PARTS = 3
PROD = PARTS * PARTS * HD
MAXROW = 96
VC = 32

DEPTH = 6
DH = 64
INNER = H * DH
WIN = 32
NP = H // 2
FF = int(P * 4 * 2 / 3)
FM = -(-FF // P)
FL = FF - (FM - 1) * P
NEG = -1.0e30


def tables():
    half = np.arange(0, DH, 2, dtype=np.float32)
    inv_freq = (np.float32(1.0) / np.power(np.float32(10000.0), half / np.float32(DH))).astype(np.float32)
    freqs = np.arange(T, dtype=np.float32)[:, None] * inv_freq[None, :]
    freqs = np.concatenate([freqs, freqs], -1).astype(np.float64)
    base = (half.astype(np.float64) + 0.4 * DH) / (1.4 * DH)
    base = np.concatenate([base, base])
    local = (np.arange(T) % P - P // 2) / (WIN // 2)
    scale = base[None, :] ** local[:, None]
    sign = np.where(np.arange(DH) < DH // 2, -1.0, 1.0)[None, :]
    cos, sin = np.cos(freqs), np.sin(freqs) * sign
    lay = lambda a: a.reshape(NT, P, DH).transpose(1, 0, 2)
    rot = np.stack([lay(cos * scale), lay(sin * scale), lay(cos / scale), lay(sin / scale)], 1)
    carry = np.tile(base ** (P / (WIN // 2)), 2)[:, None]
    i, c = np.arange(P)[:, None] % WIN, np.arange(2 * WIN)[None, :]
    ok = (i <= c) & (c <= i + WIN)
    first = ok & ~((np.arange(P)[:, None] < WIN) & (c < WIN))
    mask = np.stack([np.where(first, 0.0, NEG), np.where(ok, 0.0, NEG)], 1)
    ident = np.eye(P)
    f = lambda a: np.ascontiguousarray(a, dtype=np.float32)
    return {"rot": f(rot), "carry": f(carry), "mask": f(mask), "ident": f(ident)}


class Schedule:

    def __init__(self, nc, ctx):
        self.nc, self.ctx = nc, ctx
        self.queues = {"pe": [], "dve": [], "act": [], "pool": [], "sp": []}
        self.counts = {}
        self.sems = {}
        self.pool_last = None

    def sem(self, name):
        if name not in self.sems:
            self.sems[name] = self.ctx.enter_context(self.nc.semaphore(name))
            self.counts[name] = 0
        return name

    def step(self, engine, waits, issue, sem):
        self.sem(sem)
        self.counts[sem] += 1
        mark = (sem, self.counts[sem])
        if engine == "pool":
            waits, self.pool_last = list(waits) + [self.pool_last], mark
        self.queues[engine].append((tuple(waits), issue, sem, 1))
        return mark

    def dma(self, engine, waits, out, in_, sem):
        self.sem(sem)
        self.counts[sem] += 16
        self.queues[engine].append((tuple(waits), lambda e: e.dma_start(out, in_), sem, 16))
        return (sem, self.counts[sem])

    def play(self, engine, e):
        seen = {}
        for waits, issue, sem, inc in self.queues[engine]:
            for mark in waits:
                if mark is not None and seen.get(mark[0], 0) < mark[1]:
                    e.wait_ge(self.sems[mark[0]], mark[1])
                    seen[mark[0]] = mark[1]
            ins = issue(e)
            if inc:
                ins.then_inc(self.sems[sem], inc)


def rsqrt(s, name, shape, src, tmp, out, lo, ready):
    c, t = tmp
    op = ALU.max if lo[0] == "max" else ALU.add
    a = s.step("dve", ready, lambda e: e.tensor_scalar(c, src, lo[1], None, op), name + "_arg")
    b = s.step("act", [a], lambda e: e.activation(t, c, ACT.Ln), name + "_ln")
    b = s.step("act", [b], lambda e: e.activation(out, t, ACT.Exp, scale=-0.5), name + "_exp")
    d = s.step("dve", [b], lambda e: e.tensor_tensor(t, out, out, ALU.mult), name + "_sq")
    d = s.step("dve", [d], lambda e: e.scalar_tensor_tensor(
        out=t, in0=t, scalar=-0.5, in1=c, op0=ALU.mult, op1=ALU.mult), name + "_sq")
    return s.step("dve", [d], lambda e: e.scalar_tensor_tensor(
        out=out, in0=t, scalar=1.5, in1=out, op0=ALU.add, op1=ALU.mult), name + "_r")


def build(nc, d, out):
    with ExitStack() as ctx:
        s = Schedule(nc, ctx)
        sb = lambda c, n, shape, dt=F32: c.enter_context(nc.sbuf_tensor(n, shape, dt))
        ps = lambda c, n, shape, dt=F32: c.enter_context(nc.psum_tensor(n, shape, dt))

        x_tok = sb(ctx, "x_tok", [P, NT, P])
        att_T = sb(ctx, "att_T", [P, T])
        stream = [sb(ctx, f"stream{i}", [P, T + 1]) for i in range(2)]
        ident = sb(ctx, "ident", [P, P])
        ident_bf = sb(ctx, "ident_bf", [P, P], BF16)
        ones = sb(ctx, "ones", [P, P])
        ones_row = sb(ctx, "ones_row", [1, P])
        carry = sb(ctx, "carry", [P, 1])
        mask_f = sb(ctx, "mask_f", [P, 2, 2 * WIN])
        mask_bf = sb(ctx, "mask_bf", [P, 2, NP, 2 * WIN], BF16)

        m_x = s.dma("sp", [], x_tok[:, :, :], d["x"].rearrange("a (i p) d -> p (a i) d", p=P), "ld_x")
        m_id = s.dma("sp", [], ident[:, :], d["ident"], "ld_id")
        s.dma("sp", [], carry[:, :], d["carry"], "ld_tab")
        m_tab = s.dma("sp", [], mask_f[:, :, :], d["mask"], "ld_tab")

        m_ones = s.step("pool", [], lambda e: e.memset(ones[:, :], 1.0 / P), "const")
        m_ones = s.step("pool", [], lambda e: e.memset(ones_row[:, :], 1.0), "const")
        for i in range(2):
            m_ones = s.step("pool", [], lambda e, i=i: e.memset(stream[i][64:P, 0:1], 0.0), "const")

        with ExitStack() as phase_a:
            done_a = part_a(nc, s, phase_a, sb, ps, d, x_tok, att_T, stream, ident, ident_bf, ones_row,
                            m_x, m_id, m_ones)
        with ExitStack() as phase_b:
            done_b = part_b(nc, s, phase_b, sb, ps, d, stream, ident, ident_bf, ones, ones_row, carry,
                            mask_f, mask_bf, m_tab, m_ones, done_a)

        with ExitStack() as phase_c:
            fin = [ps(phase_c, f"fin{i}", [P, 4, P]) for i in range(2)]
            x0 = stream[0]
            s.step("dve", done_b + done_a, lambda e: e.tensor_tensor(
                att_T[0:64, :], att_T[0:64, :], x0[0:64, 0:T], ALU.add), "fin_sum")
            a = s.step("dve", [], lambda e: e.tensor_tensor(
                att_T[64:P, :], att_T[64:P, :], x0[64:P, 1:T + 1], ALU.add), "fin_sum")
            added = [None, None]
            for g in range(NC):
                def turn(e, g=g):
                    for j in range(4):
                        i = 4 * g + j
                        ins = e.transpose(fin[g % 2][:, j, :], att_T[:, i * P:(i + 1) * P], ident[:, :])
                    return ins
                m = s.step("pe", [a, added[-2]] + done_b, turn, "fin_T")
                tok = x_tok[:, 4 * g:4 * g + 4, :]
                added.append(s.step("dve", [m], lambda e, g=g, tok=tok: e.tensor_tensor(
                    tok, fin[g % 2][:, :, :], tok, ALU.add), "fin_add"))
                m_out = s.dma("sp", [added[-1]], out.rearrange("a (i p) d -> p (a i) d", p=P)[:, 4 * g:4 * g + 4, :],
                              tok, "st_out")
        sems = s.sems
        block = ctx.enter_context(nc.Block())

        @block.sync
        def _(e):
            s.play("sp", e)
            e.wait_ge(sems[m_out[0]], m_out[1])

        @block.gpsimd
        def _(e):
            s.play("pool", e)

        @block.scalar
        def _(e):
            s.play("act", e)

        @block.vector
        def _(e):
            s.play("dve", e)

        @block.tensor
        def _(e):
            s.play("pe", e)


def part_a(nc, s, ctx, sb, ps, d, x_tok, att_T, stream, ident, ident_bf, ones_row, m_x, m_id, m_ones):
    w_raw = {n: sb(ctx, "w_" + n, [P, P]) for n in ("Wq", "Wk", "Wv", "Wo")}
    b_col = {n: sb(ctx, "b_" + n, [P, 1]) for n in ("bq", "bk", "bv", "bo")}
    bdV = sb(ctx, "bdV", [P, P])
    bdU = sb(ctx, "bdU", [P, P])
    xn_T = sb(ctx, "xn_T", [P, T])
    xc = sb(ctx, "xc", [P, NT, P])
    sq = sb(ctx, "sqA", [P, NT, P])
    stat = sb(ctx, "statA", [P, 6, NT])
    w_z = {n: sb(ctx, "wz_" + n, [P, P]) for n in ("Wq", "Wk", "Wv")}
    b_z = {n: sb(ctx, "bz_" + n, [P, 1]) for n in ("bq", "bk")}
    bv_row = sb(ctx, "bv_row", [1, P])
    wo_T = sb(ctx, "wo_T", [P, P])
    w_out = sb(ctx, "w_out", [P, P])
    z = {n: sb(ctx, "z_" + n, [P, T]) for n in "qk"}
    zp = {n: sb(ctx, "zp_" + n, [P, PARTS, T], BF16) for n in "qk"}
    va = sb(ctx, "va", [P, NT, H, VC])
    QS = [sb(ctx, f"QS{i}", [P, T], BF16) for i in range(3)]
    KS = [sb(ctx, f"KS{i}", [P, T], BF16) for i in range(3)]
    mx = [sb(ctx, f"mx{i}", [P, NT, 2]) for i in range(2)]
    nmax = [sb(ctx, f"nmax{i}", [P, NT]) for i in range(2)]
    nm_r = sb(ctx, "nm_r", [NT, P])
    nm_p = [sb(ctx, f"nm_p{i}", [NT, PARTS, P], BF16) for i in range(2)]
    NPT = 8
    PT = [sb(ctx, f"PT{i}", [P, CH]) for i in range(NPT)]
    o_h = [sb(ctx, f"o_h{i}", [P, CH]) for i in range(2)]
    y = z["q"]
    l = z["k"]
    S_ps = [ps(ctx, f"S_ps{i}", [P, 2, CH]) for i in range(2)]
    E_ps = [ps(ctx, f"E_ps{i}", [P, CH]) for i in range(2)]
    O_ps = ps(ctx, "O_ps", [P, CH])
    M_ps = ps(ctx, "M_ps", [P, CH])

    for n in w_raw:
        m_w = s.dma("sp", [], w_raw[n][:, :], d[n], "ld_w")
    for n in b_col:
        m_w = s.dma("sp", [], b_col[n][:, :], d[n].rearrange("(p o) -> p o", o=1), "ld_w")
    m_z = s.step("pool", [], lambda e: e.memset(bdV[:, :], 0.0), "zeroA")
    m_z = s.step("pool", [], lambda e: e.memset(bdU[:, :], 0.0), "zeroA")
    for h in range(H):
        b = slice(h * HD, (h + 1) * HD)
        s.dma("sp" if h % 2 else "act", [m_z], bdV[b, b], d["V"], "ld_bd")
        m_bd = s.dma("act" if h % 2 else "sp", [m_z], bdU[b, b], d["U"], "ld_bd")
    m_va = s.step("pool", [], lambda e: e.memset(va[:, :, :, :], 1.0), "zeroA")
    for i in range(3):
        s.step("pool", [], lambda e, i=i: e.memset(QS[i][64:P, :], 0.0), "zeroA")
        m0 = s.step("pool", [], lambda e, i=i: e.memset(KS[i][64:P, :], 0.0), "zeroA")
        m_st = s.step("pool", [m0], lambda e, i=i: e.memset(KS[i][MAXROW:MAXROW + PARTS, :], 1.0), "zeroA")
    m_idb = s.step("dve", [m_id], lambda e: e.tensor_copy(ident_bf[:, :], ident[:, :]), "idb")

    s.queues["act"].append(((), lambda e: e.preload_act_table_set("natural_log_exp_and_others"), None, 0))
    bc = lambda a: a.unsqueeze(2).to_broadcast([P, NT, P])
    mean, var = stat[:, 0, :], stat[:, 1, :]
    a = s.step("dve", [m_x], lambda e: e.tensor_reduce(mean, x_tok[:, :, :], AX.X, ALU.add), "lnA")
    a = s.step("dve", [a], lambda e: e.tensor_scalar(mean, mean, 1.0 / P, None, ALU.mult), "lnA")
    a = s.step("dve", [a], lambda e: e.tensor_tensor(xc[:, :, :], x_tok[:, :, :], bc(mean), ALU.subtract), "lnA")
    a = s.step("dve", [a], lambda e: e.tensor_tensor(sq[:, :, :], xc[:, :, :], xc[:, :, :], ALU.mult), "lnA")
    a = s.step("dve", [a], lambda e: e.tensor_reduce(var, sq[:, :, :], AX.X, ALU.add), "lnA")
    a = s.step("dve", [a], lambda e: e.tensor_scalar(var, var, 1.0 / P, None, ALU.mult), "lnA")
    r = rsqrt(s, "rA", None, var, (stat[:, 2, :], stat[:, 3, :]), stat[:, 4, :], ("add", 1e-5), [a])
    m_xn = s.step("dve", [r], lambda e: e.tensor_tensor(sq[:, :, :], xc[:, :, :], bc(stat[:, 4, :]), ALU.mult), "lnA")

    scale = 1.0 / float(np.sqrt(np.float32(HD)))
    banks = [S_ps[0][:, 0, :], S_ps[0][:, 1, :], S_ps[1][:, 0, :], S_ps[1][:, 1, :], E_ps[0][:, :], E_ps[1][:, :],
             O_ps[:, :], M_ps[:, :]]
    free = [None] * 8
    turn_n = [0]

    def bank():
        turn_n[0] = (turn_n[0] + 1) % 8
        return turn_n[0]

    def small(waits, mm, evac, sem):
        b = bank()
        m = s.step("pe", waits + [free[b]], lambda e: mm(e, banks[b]), sem + "_mm")
        free[b] = s.step("dve", [m], lambda e: evac(e, banks[b]), sem)
        return free[b]

    for n in ("Wq", "Wk", "Wv"):
        k = scale if n == "Wq" else 1.0
        m_wz = small([m_w, m_bd], lambda e, b, n=n: e.matmul(b[:, 0:P], w_raw[n][:, :], bdV[:, :], start=True, stop=True),
                     lambda e, b, n=n, k=k: e.tensor_scalar(w_z[n][:, :], b[:, 0:P], k, None, ALU.mult), "fold")
    for n in ("bq", "bk"):
        k = scale if n == "bq" else 1.0
        m_wz = small([], lambda e, b, n=n: e.matmul(b[:, 0:1], bdV[:, :], b_col[n][:, :], start=True, stop=True),
                     lambda e, b, n=n, k=k: e.tensor_scalar(b_z[n][:, :], b[:, 0:1], k, None, ALU.mult), "fold")
    m_wz = small([], lambda e, b: e.matmul(b[0:1, 0:P], b_col["bv"][:, :], bdV[:, :], start=True, stop=True),
                 lambda e, b: e.tensor_copy(bv_row[:, :], b[0:1, 0:P]), "fold")
    m_wt = small([m_id], lambda e, b: e.transpose(b[:, 0:P], w_raw["Wo"][:, :], ident[:, :]),
                 lambda e, b: e.tensor_copy(wo_T[:, :], b[:, 0:P]), "fold")
    m_wz = small([m_wt], lambda e, b: e.matmul(b[:, 0:P], bdU[:, :], wo_T[:, :], start=True, stop=True),
                 lambda e, b: e.tensor_copy(w_out[:, :], b[:, 0:P]), "fold")

    for g in range(NC):
        def turn(e, bk, g=g):
            for j in range(4):
                ins = e.transpose(bk[:, j * P:(j + 1) * P], sq[:, 4 * g + j, :], ident[:, :])
            return ins
        b = bank()
        m = s.step("pe", [m_xn, m_id, free[b]], lambda e, b=b, t=turn: t(e, banks[b]), "xT_mm")
        c = slice(g * CH, (g + 1) * CH)
        free[b] = s.step("act", [m], lambda e, b=b, c=c: e.activation(xn_T[:, c], banks[b], ACT.Copy), "xT")
        s.step("pool", [free[b]], lambda e, c=c: e.tensor_copy(stream[0][0:64, c], xn_T[0:64, c]), "skew")
        m_skew = s.step("pool", [], lambda e, c=c, g=g: e.tensor_copy(
            stream[0][64:P, g * CH + 1:(g + 1) * CH + 1], xn_T[64:P, c]), "skew")
        m_xT = free[b]

    m_part = {}
    for n, w, bz in (("q", "Wq", "bq"), ("k", "Wk", "bk")):
        for g in range(NC):
            c = slice(g * CH, (g + 1) * CH)
            b = bank()
            m = s.step("pe", [m_xT, m_wz, free[b]], lambda e, b=b, c=c, w=w: e.matmul(
                banks[b], w_z[w][:, :], xn_T[:, c], start=True, stop=True), "z_mm")
            free[b] = s.step("act", [m], lambda e, b=b, c=c, n=n, bz=bz: e.activation(
                z[n][:, c], banks[b], ACT.Identity, bias=b_z[bz][:, 0:1]), "z")
        a = free[b]
        for i in range(PARTS):
            a = s.step("dve", [a], lambda e, n=n, i=i: e.tensor_copy(zp[n][:, i, :], z[n][:, :]), "part")
            if i < PARTS - 1:
                a = s.step("dve", [a], lambda e, n=n, i=i: e.tensor_tensor(
                    z[n][:, :], z[n][:, :], zp[n][:, i, :], ALU.subtract), "part")
        m_part[n] = a

    for g in range(NC):
        def vals(e, bk, g=g):
            for j in range(4):
                i = 4 * g + j
                e.matmul(bk[:, j * P:(j + 1) * P], xn_T[:, i * P:(i + 1) * P], w_z["Wv"][:, :],
                         start=(j == 0), stop=False, skip_group_check=True)
                ins = e.matmul(bk[:, j * P:(j + 1) * P], ones_row[:, :], bv_row[:, :],
                               start=False, stop=True, skip_group_check=True)
            return ins
        b = bank()
        m = s.step("pe", [free[b], m_ones], lambda e, b=b, f=vals: f(e, banks[b]), "v_mm")
        free[b] = s.step("act", [m, m_va], lambda e, b=b, g=g: e.activation(
            va[:, 4 * g:4 * g + 4, :, 0:HD],
            banks[b].rearrange("p (j h d) -> p j h d", j=4, h=H), ACT.Copy), "va")
        m_vals = free[b]

    m_stack = {}
    m_pass1 = {}
    m_pass2 = {}
    reads = []
    exps = []
    pvs = []
    m_nrow = {}
    m_oev = {}
    m_tr = {}
    m_nmdma = {}
    m_odma = {}

    def stack(h):
        sl = h % 3
        w = [m_part["q"], m_part["k"], m_st, m_pass2.get(h - 3)]
        rows = slice(h * HD, (h + 1) * HD)
        for i in range(PARTS):
            for j in range(PARTS):
                to = slice((PARTS * i + j) * HD, (PARTS * i + j + 1) * HD)
                s.dma("sp", w, QS[sl][to, :], zp["q"][rows, i, :], f"ld_stack{sl}")
                m_stack[h] = s.dma("sp", w, KS[sl][to, :], zp["k"][rows, j, :], f"ld_stack{sl}")

    def scores(h, i, hf):
        sl, n = h % 3, len(reads)
        def mm(e):
            for c in range(2):
                k = (2 * hf + c) * CH
                ins = e.matmul(S_ps[n % 2][:, c, :], QS[sl][0:MAXROW, i * P:(i + 1) * P],
                               KS[sl][0:MAXROW, k:k + CH], start=True, stop=True)
            return ins
        m = s.step("pe", [m_stack[h], reads[n - 2] if n >= 2 else free_all], mm, "sc_mm")
        reads.append(s.step("dve", [m, m_tr.get(h - 2)], lambda e: e.tensor_reduce(
            mx[h % 2][:, i, hf:hf + 1], S_ps[n % 2][:, :, :], AX.XY, ALU.max), "sc_max"))

    def max_rows(h):
        sl, b = h % 3, h % 2
        a = s.step("dve", [reads[-1]], lambda e: e.tensor_reduce(nmax[b][:, :], mx[b][:, :, :], AX.X, ALU.max, negate=True), "nm")
        m_tr[h] = a
        a = s.step("pe", [a, m_nrow.get(h - 1), m_id], lambda e: e.transpose(M_ps[0:NT, 0:P], nmax[b][:, :], ident[:, :]), "nm_T")
        a = s.step("dve", [a], lambda e: e.tensor_copy(nm_r[:, :], M_ps[0:NT, 0:P]), "nm")
        m_nrow[h] = a
        for i in range(PARTS):
            a = s.step("dve", [a, m_nmdma.get(h - 2)], lambda e, i=i: e.tensor_copy(nm_p[b][:, i, :], nm_r[:, :]), "nm")
            if i < PARTS - 1:
                a = s.step("dve", [a], lambda e, i=i: e.tensor_tensor(nm_r[:, :], nm_r[:, :], nm_p[b][:, i, :], ALU.subtract), "nm")
        for i in range(PARTS):
            m_nmdma[h] = s.dma("sp", [a, m_pass2.get(h - 3)], QS[sl][MAXROW + i:MAXROW + i + 1, :], nm_p[b][:, i, :], f"ld_max{b}")

    def probs(h, j, c):
        sl, n = h % 3, len(exps)
        m = s.step("pe", [m_nmdma[h], exps[n - 2] if n >= 2 else free_all], lambda e: e.matmul(
            E_ps[n % 2][:, :], KS[sl][0:MAXROW + PARTS, j * P:(j + 1) * P],
            QS[sl][0:MAXROW + PARTS, c * CH:(c + 1) * CH], start=True, stop=True), "pr_mm")
        exps.append(s.step("act", [m, pvs[n - NPT] if n >= NPT else None], lambda e: e.activation(
            PT[n % NPT][:, :], E_ps[n % 2][:, :], ACT.Exp), "pr_exp"))
        m_pass2[h] = m

    def values(h, j):
        for c in range(NC):
            n = len(pvs)
            pvs.append(s.step("pe", [exps[n], m_vals, m_oev.get(h - 1)] if j == 0 else [exps[n]],
                              lambda e, c=c, n=n: e.matmul(
                O_ps[VC * c:VC * (c + 1), :], va[:, j, h, :], PT[n % NPT][:, :], start=(j == 0), stop=(j == NT - 1)), "pv"))
        if j == NT - 1:
            b = h % 2
            m_oev[h] = s.step("dve", [pvs[-1], m_odma.get(h - 2)], lambda e: e.tensor_copy(o_h[b][:, :], O_ps[:, :]), "o_ev")
            rows = slice(h * HD, (h + 1) * HD)
            for c in range(NC):
                s.dma("sp", [m_oev[h], m_part["q"]], y[rows, c * CH:(c + 1) * CH], o_h[b][VC * c:VC * c + HD, :], f"ld_o{b}")
                m_odma[h] = s.dma("sp", [m_oev[h], m_part["k"]], l[rows, c * CH:(c + 1) * CH], o_h[b][VC * c + HD:VC * c + 2 * HD, :], f"ld_o{b}")

    free_all = s.step("pe", free, lambda e: e.matmul(M_ps[0:1, 0:1], ones_row[0:1, 0:1], ones_row[0:1, 0:1], start=True, stop=True), "prep")
    AHEAD = NT + NT // 2
    stack(0)
    stack(1)
    last_values = None
    for u in range(H * NT + AHEAD):
        n, k = u, u - AHEAD
        mh, mi = divmod(n, NT)
        eh, ej = divmod(k, NT)
        if k >= 0 and ej == 0 and eh + 2 < H:
            stack(eh + 2)
        for c in range(NC):
            if k >= 0:
                probs(eh, ej, c)
            if mh < H and c % 2 == 0:
                scores(mh, mi, c // 2)
            if last_values and c == 1:
                values(*last_values)
        if mh < H and mi == NT - 1:
            max_rows(mh)
        last_values = (eh, ej) if k >= 0 else None
    values(*last_values)

    a = s.step("dve", [m_odma[H - 1], m_odma[H - 2]], lambda e: e.reciprocal(l[:, :], l[:, :]), "norm")
    a = s.step("dve", [a], lambda e: e.tensor_tensor(y[:, :], y[:, :], l[:, :], ALU.mult), "norm")
    for g in range(NC):
        c = slice(g * CH, (g + 1) * CH)
        bk = banks[g]
        m = s.step("pe", [a, reads[-1], reads[-2], exps[-1], exps[-2]], lambda e, bk=bk, c=c: e.matmul(bk, w_out[:, :], y[:, c], start=True, stop=True), "att_mm")
        m_att = s.step("act", [m], lambda e, bk=bk, c=c: e.activation(att_T[:, c], bk, ACT.Identity, bias=b_col["bo"][:, 0:1]), "att")
    return [m_att, m_skew, pvs[-1], m_oev[H - 1], m_odma[H - 1], m_odma[H - 2], m_part["k"], m_idb]


def part_b(nc, s, ctx, sb, ps, d, stream, ident, ident_bf, ones, ones_row, carry, mask_f, mask_bf, m_tab, m_ones, done_a):
    w_qkv = sb(ctx, "w_qkv", [P, 3 * INNER])
    w_o = sb(ctx, "w_o", [P, NP, P])
    w_1 = sb(ctx, "w_1", [P, 2 * FF])
    w_2 = sb(ctx, "w_2", [P, FM, P])
    b_1 = sb(ctx, "b_1", [P, 2, FM])
    cols = sb(ctx, "cols", [P, 3])
    rot = sb(ctx, "rot", [P, 4, NT, DH])
    gains = sb(ctx, "gains", [P, 2, DH])
    sq = sb(ctx, "sq", [P, INNER])
    ss = [sb(ctx, f"ss{i}", [P, 2 * H]) for i in range(2)]
    rs = [[sb(ctx, f"rs{i}{j}", [P, 2 * H]) for j in range(3)] for i in range(2)]
    nrm = [sb(ctx, f"nrm{i}", [P, INNER]) for i in range(2)]
    tcs = [[sb(ctx, f"tc{i}{j}", [P, INNER]) for i in range(2)] for j in range(2)]
    ts = [sb(ctx, f"ts{i}", [P, INNER]) for i in range(2)]
    q_T = sb(ctx, "q_T", [P, NP, P])
    k_T = [sb(ctx, f"k_T{i}", [P, NP, WIN + P]) for i in range(2)]
    NV = 4
    v_all = sb(ctx, "v_all", [P, NV, INNER])
    v = [v_all[:, i, :] for i in range(NV)]
    v_sh = [sb(ctx, f"v_sh{i}", [P, INNER]) for i in range(2)]
    pr = [sb(ctx, f"pr{i}", [P, H, 2 * WIN]) for i in range(2)]
    pc = sb(ctx, "pc", [P, H, 2 * WIN])
    mx = sb(ctx, "mxB", [P, 3, H])
    pT = [sb(ctx, f"pT{i}", [P, H, P]) for i in range(2)]
    o_T = [sb(ctx, f"o_T{i}", [P, NP, P]) for i in range(2)]
    xl = sb(ctx, "xl", [P, T])
    lnb = sb(ctx, "lnb", [P, CH])
    row = sb(ctx, "row", [1, 4, CH])
    hid = v_all[:, :, :].rearrange("p a (b c) -> p (a b) c", c=CH)
    gel = [sb(ctx, f"gel{i}", [P, CH]) for i in range(2)]
    W_ps = [ps(ctx, f"W_ps{i}", [P, 2, CH]) for i in range(2)]
    T_ps = [ps(ctx, f"T_ps{i}", [P, 4, P]) for i in range(2)]
    S_ps = ps(ctx, "SB_ps", [P, 2, NP, 2 * WIN])

    m_mask = s.step("dve", [m_tab] + done_a, lambda e: e.tensor_copy(
        mask_bf[:, :, :, :], mask_f[:, :, :].unsqueeze(2).to_broadcast([P, 2, NP, 2 * WIN])), "mask")
    for i in range(2):
        s.step("pool", done_a, lambda e, i=i: e.memset(pT[i][:, :, :], 0.0), "zeroB")
        s.step("pool", [], lambda e, i=i: e.memset(v_sh[i][0:WIN, :], 0.0), "zeroB")
        m_zero = s.step("pool", [], lambda e, i=i: e.memset(k_T[i][:, :, 0:WIN], 0.0), "zeroB")

    def table(name):
        s.queues["act"].append(((), lambda e: e.preload_act_table_set(name), None, 0))

    last = {}

    def L(*names):
        return [last.get(n) for n in names]

    t_uses = []
    x_in, x_out = stream
    x_ready = [done_a] * NC
    w_uses = []

    def load_attn(n):
        w = done_a + L("proj_mm", "y_mm")
        for j in range(3):
            c = slice(j * INNER, (j + 1) * INNER)
            last["w_qkv"] = s.dma("sp", w, w_qkv[:, c], d["Wqkv"][n][:, c], "ld_wqkv")
        last["w_o"] = s.dma("sp", w, w_o[:, :, :], d["Wo2"][n].rearrange("(k p) n -> p k n", p=P), "ld_wo")
        w = done_a + L("rot_use_d", "rot_use_p")
        s.dma("sp", w, rot[:, :, :, :], d["rot"], "ld_rot")
        s.dma("sp", w, gains[:, 0, :], d["q_scale"][n:n + 1, :].to_broadcast([P, DH]), "ld_rot")
        m = s.dma("sp", w, gains[:, 1, :], d["k_scale"][n:n + 1, :].to_broadcast([P, DH]), "ld_rot")
        HF = DH // 2
        for i in range(2):
            g = gains[:, i, :]
            b = lambda a, k: a.unsqueeze(1).to_broadcast([P, NT, k])
            s.step("pool", [m], lambda e, i=i, g=g: e.tensor_tensor(rot[:, 2 * i, :, :], rot[:, 2 * i, :, :], b(g, DH), ALU.mult), "rot")
            s.step("pool", [m], lambda e, i=i, g=g: e.tensor_tensor(
                rot[:, 2 * i + 1, :, 0:HF], rot[:, 2 * i + 1, :, 0:HF], b(g[:, HF:DH], HF), ALU.mult), "rot")
            last["rot"] = s.step("pool", [m], lambda e, i=i, g=g: e.tensor_tensor(
                rot[:, 2 * i + 1, :, HF:DH], rot[:, 2 * i + 1, :, HF:DH], b(g[:, 0:HF], HF), ALU.mult), "rot")

    def load_mlp(n):
        w = done_a + L("up_mm", "down_mm", "ffn_dve", "gelu")
        s.dma("sp", w, w_1[:, :], d["W1"][n], "ld_mlp")
        s.dma("sp", w, w_2[:, 0:FM - 1, :], d["W2"][n][0:(FM - 1) * P, :].rearrange("(k p) n -> p k n", p=P), "ld_mlp")
        s.dma("sp", w, w_2[0:FL, FM - 1, :], d["W2"][n][(FM - 1) * P:FF, :], "ld_mlp")
        for i in range(2):
            o = i * FF
            b = d["b1"][n]
            for k in range(FM):
                m = P if k < FM - 1 else FL
                s.dma("sp", w, b_1[0:m, i, k:k + 1], b[o + k * P:o + k * P + m].rearrange("(p o) -> p o", o=1), "ld_mlp")
        for i, nme in enumerate(("ln_g", "ln_b", "b2")):
            last["mlp_w"] = s.dma("sp", w, cols[:, i:i + 1], d[nme][n].rearrange("(p o) -> p o", o=1), "ld_mlp")

    def project(tile, which):
        n = len(w_uses)
        c = tile * P // CH
        def mm(e, tile=tile, which=which, n=n):
            for hf in range(2):
                o = which * INNER + hf * CH
                ins = e.matmul(W_ps[n % 2][:, hf, :], x_in[:, tile * P:(tile + 1) * P], w_qkv[:, o:o + CH],
                               start=True, stop=True)
            return ins
        m = s.step("pe", list(x_ready[c]) + L("w_qkv") + [w_uses[n - 2] if n >= 2 else None], mm, "proj")
        last["proj_mm"] = m
        w_uses.append(None)
        return n, m

    def norms(tile, pn):
        st = tile % 2
        for i, (n, m) in enumerate(pn):
            a = s.step("act", [m, last.get("ss_red")], lambda e, n=n: e.activation(
                sq[:, :].rearrange("p (a b) -> p a b", a=2), W_ps[n % 2][:, :, :], ACT.Square), "sq")
            last["ss_red"] = s.step("dve", [a, last.get(("rs", st))], lambda e, i=i, st=st: e.tensor_reduce(
                ss[st][:, i * H:(i + 1) * H], sq[:, :].rearrange("p (h d) -> p h d", h=H), AX.X, ALU.add), "ss")
        r = rs[st]
        m_r = rsqrt(s, "rB", None, ss[st][:, :], (r[0][:, :], r[1][:, :]), r[2][:, :], ("max", 1e-24), [last["ss_red"]])
        last[("rs", st)] = m_r
        return m_r

    def rotate(tile, pn, m_r):
        st = tile % 2
        tc = tcs[st]
        HF = DH // 2
        marks = []
        for i, (n, m) in enumerate(pn):
            view = lambda a: a.rearrange("p (h d) -> p h d", h=H)
            a = s.step("dve", [m_r, last.get(("nrm", i))], lambda e, i=i, n=n: e.tensor_tensor(
                view(nrm[i][:, :]), W_ps[n % 2][:, :, :].rearrange("p a (h d) -> p (a h) d", d=DH),
                rs[st][2][:, i * H:(i + 1) * H].unsqueeze(2).to_broadcast([P, H, DH]), ALU.mult), "nrm")
            w_uses[n] = a
            eng = "dve" if i == 0 else "pool"
            cosn, sinn = rot[:, 2 * i, tile, :], rot[:, 2 * i + 1, tile, :]
            b = lambda t, k: t.unsqueeze(1).to_broadcast([P, H, k])
            s.step(eng, [a, last.get("rot"), last.get(("tc", i, st))], lambda e, i=i, c=cosn: e.tensor_tensor(
                view(tc[i][:, :]), view(nrm[i][:, :]), b(c, DH), ALU.mult), f"trig{i}")
            s.step(eng, [a, last.get(("ts", i))], lambda e, i=i, c=sinn: e.tensor_tensor(
                view(ts[i][:, :])[:, :, 0:HF], view(nrm[i][:, :])[:, :, HF:DH], b(c[:, 0:HF], HF), ALU.mult), f"trig{i}")
            a = s.step(eng, [a], lambda e, i=i, c=sinn: e.tensor_tensor(
                view(ts[i][:, :])[:, :, HF:DH], view(nrm[i][:, :])[:, :, 0:HF], b(c[:, HF:DH], HF), ALU.mult), f"trig{i}")
            last[("nrm", i)] = a
            last["rot_use_d" if i == 0 else "rot_use_p"] = a
            a = s.step("pool", [a], lambda e, i=i: e.tensor_tensor(tc[i][:, :], tc[i][:, :], ts[i][:, :], ALU.add), "rotsum")
            last[("ts", i)] = a
            marks.append(a)
        return marks

    def turn(tile, rotated):
        tc = tcs[tile % 2]
        for i in range(2):
            for hf in range(2):
                n = len(t_uses)
                def tr(e, i=i, hf=hf, n=n):
                    for j in range(4):
                        b = 4 * hf + j
                        ins = e.transpose(T_ps[n % 2][:, j, :], tc[i][:, b * P:(b + 1) * P], ident[:, :])
                    return ins
                m = s.step("pe", [rotated[i], t_uses[n - 2] if n >= 2 else None], tr, "turn_mm")
                pslot = slice(4 * hf, 4 * hf + 4)
                if i == 0:
                    a = s.step("act", [m, last.get("score")], lambda e, n=n, pslot=pslot: e.activation(
                        q_T[:, pslot, :], T_ps[n % 2][:, :, :], ACT.Copy), "turn")
                else:
                    kt, kn = k_T[tile % 2], k_T[(tile + 1) % 2]
                    s.step("act", [m, last.get(("k", tile % 2)), m_zero], lambda e, n=n, pslot=pslot, kt=kt: e.activation(
                        kt[:, pslot, WIN:WIN + P], T_ps[n % 2][:, :, :], ACT.Copy), "turn")
                    a = s.step("act", [last.get(("k", (tile + 1) % 2))], lambda e, n=n, pslot=pslot, kn=kn: e.activation(
                        kn[:, pslot, 0:WIN], T_ps[n % 2][:, :, P - WIN:P], ACT.Copy, scale=carry[:, 0:1]), "turn")
                t_uses.append(a)
            last[("tc", i, tile % 2)] = m
        return a

    v_marks = {}

    def keep_v(tile, n, m):
        if tile == 0:
            v_marks.clear()
        sl = v[tile % NV]
        a = s.step("act", [m, v_marks.get(("use", tile - NV)), v_marks.get(("sh", tile - NV)), v_marks.get(("sh", tile - NV + 1)), last.get("down_mm")],
                   lambda e, n=n, sl=sl: e.activation(
            sl[:, :].rearrange("p (a b) -> p a b", a=2), W_ps[n % 2][:, :, :], ACT.Copy), "v")
        w_uses[n] = a
        v_marks[("v", tile)] = a

    def shift_v(tile):
        sl, sh = v[tile % NV], v_sh[tile % 2]
        w = [v_marks[("v", tile)], v_marks.get(("use", tile - 2)), m_zero]
        key = f"ld_vsh{tile % 2}"
        b = s.dma("sp", w, sh[WIN:P, :], sl[0:P - WIN, :], key)
        if tile:
            b = s.dma("sp", w, sh[0:WIN, :], v[(tile - 1) % NV][P - WIN:P, :], key)
        v_marks[("sh", tile)] = b

    def score(tile, m_kq):
        kt = k_T[tile % 2]
        mk = mask_bf[:, 0 if tile == 0 else 1, :, :]
        def mm(e, kt=kt, mk=mk):
            for par in range(2):
                e.matmul(S_ps[:, par, :, :], ident_bf[:, :], mk, start=True, stop=False, skip_group_check=True)
            for p in range(NP):
                for par in range(2):
                    r = slice(DH * par, DH * (par + 1))
                    for w in range(P // WIN):
                        ins = e.matmul(S_ps[WIN * w:WIN * (w + 1), par, p, :], q_T[r, p, WIN * w:WIN * (w + 1)],
                                       kt[r, p, WIN * w:WIN * w + 2 * WIN], start=False, stop=True, skip_group_check=True)
            return ins
        m = s.step("pe", [m_kq, m_mask, last.get("s_read")], mm, "score_mm")
        last["score"] = m
        last[("k", tile % 2)] = m
        pb = pr[tile % 2]
        sv = S_ps[:, :, :, :].rearrange("p a b c -> p (a b) c")
        bc = lambda a: a.unsqueeze(2).to_broadcast([P, H, 2 * WIN])
        a = s.step("dve", [m], lambda e: e.tensor_reduce(mx[:, 0, :], sv, AX.X, ALU.max), "sm")
        a = s.step("dve", [a, last.get(("pr", tile % 2))], lambda e: e.tensor_tensor(pb[:, :, :], sv, bc(mx[:, 0, :]), ALU.subtract), "sm")
        last["s_read"] = a
        a = s.step("act", [a], lambda e: e.activation(pb[:, :, :], pb[:, :, :], ACT.Exp, scale=8.0), "smexp")
        a = s.step("dve", [a, last.get("p_norm")], lambda e: e.tensor_reduce(mx[:, 1, :], pb[:, :, :], AX.X, ALU.add), "sm")
        a = s.step("dve", [a], lambda e: e.reciprocal(mx[:, 2, :], mx[:, 1, :]), "sm")
        a = s.step("pool", [a], lambda e: e.tensor_tensor(pb[:, :, :], pb[:, :, :], bc(mx[:, 2, :]), ALU.mult), "pnorm")
        last["p_norm"] = a
        return a

    def blocks(tile, m_p):
        pb = pr[tile % 2]
        a = s.step("dve", [m_p, last.get("pT")], lambda e: e.transpose(pc[:, :, :], pb[:, :, :]), "pT")
        last[("pr", tile % 2)] = a
        for w in range(P // WIN):
            r = slice(WIN * w, WIN * (w + 1))
            for i in range(2):
                a2 = s.step("act", [a, last.get("pv"), m_zero], lambda e, r=r, i=i: e.activation(
                    pT[i][r, :, r.start:r.stop], pc[r, :, WIN * i:WIN * (i + 1)], ACT.Copy), "pD")
        last["pT"] = a2
        return a2

    def values(tile, m_p):
        ot = o_T[tile % 2]
        for hf in range(2):
            n = len(t_uses)
            def mm(e, hf=hf, n=n, tile=tile):
                for j in range(4):
                    p = 4 * hf + j
                    for i in range(2):
                        vv = (v_sh[tile % 2], v[tile % NV])[i]
                        for par in range(2):
                            f = (2 * p + par) * DH
                            ins = e.matmul(T_ps[n % 2][DH * par:DH * (par + 1), j, :], vv[:, f:f + DH],
                                           pT[i][:, par * NP + p, :], start=(j == 0 and i == 0), stop=(i == 1), skip_group_check=True)
                return ins
            m = s.step("pe", [m_p, v_marks[("sh", tile)], v_marks[("v", tile)], t_uses[n - 2]], mm, "pv_mm")
            a = s.step("act", [m, last.get(("o", tile % 2))], lambda e, n=n, hf=hf: e.activation(
                ot[:, 4 * hf:4 * hf + 4, :], T_ps[n % 2][:, :, :], ACT.Copy), "o_T")
            t_uses.append(a)
        last["pv"] = m
        v_marks[("use", tile)] = m
        return a

    def output(tile, a):
        ot = o_T[tile % 2]
        n = len(t_uses)
        def out(e, n=n):
            for p in range(NP):
                ins = e.matmul(T_ps[n % 2][:, 0, :], w_o[:, p, :], ot[:, p, :], start=(p == 0), stop=(p == NP - 1))
            return ins
        m = s.step("pe", [a, last["w_o"], t_uses[n - 2]], out, "y_mm")
        last["y_mm"] = m
        last[("o", tile % 2)] = m
        c0 = tile * P
        s.step("dve", [m] + list(x_ready[c0 // CH]), lambda e, n=n: e.tensor_tensor(
            x_out[0:64, c0:c0 + P], T_ps[n % 2][0:64, 0, :], x_in[0:64, c0:c0 + P], ALU.add), "resid")
        a = s.step("dve", [], lambda e, n=n: e.tensor_tensor(
            x_out[64:P, c0 + 1:c0 + P + 1], T_ps[n % 2][64:P, 0, :], x_in[64:P, c0 + 1:c0 + P + 1], ALU.add), "resid")
        t_uses.append(a)
        return a

    def mlp(m_res):
        SB = S_ps[:, :, :, :].rearrange("p a b c -> p a (b c)")
        xl_ready, r_marks = [], []
        for g in range(NC):
            c = slice(g * CH, (g + 1) * CH)
            n = len(t_uses)
            tp = T_ps[n % 2][:, :, :].rearrange("p a b -> p (a b)")
            m = s.step("pe", [m_res, t_uses[n - 2]], lambda e, c=c, tp=tp: e.matmul(tp, ones[:, :], x_out[:, c], start=True, stop=True), "mean_mm")
            a = s.step("dve", [m, last.get("xl")], lambda e, c=c, tp=tp: e.tensor_tensor(xl[:, c], x_out[:, c], tp, ALU.subtract), "xc")
            t_uses.append(a)
            q = s.step("act", [a, last.get("var_mm")], lambda e, c=c: e.activation(lnb[:, :], xl[:, c], ACT.Square), "lnsq")
            n = len(t_uses)
            tv = T_ps[n % 2][0:1, :, :].rearrange("p a b -> p (a b)")
            m = s.step("pe", [q, t_uses[n - 2]], lambda e, tv=tv: e.matmul(tv, ones[:, 0:1], lnb[:, :], start=True, stop=True), "var_mm")
            last["var_mm"] = m
            r = rsqrt(s, "rL", None, tv, (row[:, 0, :], row[:, 1, :]), row[:, 2, :], ("add", 1e-5), [m, last.get("bc_mm")])
            t_uses.append(r)
            n = len(t_uses)
            tb = T_ps[n % 2][:, :, :].rearrange("p a b -> p (a b)")
            m = s.step("pe", [r, t_uses[n - 2]], lambda e, tb=tb: e.matmul(tb, ones_row[:, :], row[:, 2, :], start=True, stop=True), "bc_mm")
            last["bc_mm"] = m
            a = s.step("dve", [m], lambda e, c=c, tb=tb: e.tensor_tensor(xl[:, c], xl[:, c], tb, ALU.mult), "xc")
            t_uses.append(a)
            a = s.step("dve", [a, last["mlp_w"]], lambda e, c=c: e.tensor_scalar(
                xl[:, c], xl[:, c], cols[:, 0:1], cols[:, 1:2], ALU.mult, ALU.add), "xc")
            xl_ready.append(a)
        banks = [W_ps[0][:, 0, :], W_ps[0][:, 1, :], W_ps[1][:, 0, :], W_ps[1][:, 1, :]]
        bk_free = [w_uses[-1], w_uses[-1], w_uses[-1], w_uses[-1]]
        bk_free = [[w_uses[-1], w_uses[-2]] for _ in range(4)]
        new = []
        k_n = 0
        for g in range(NC):
            c = slice(g * CH, (g + 1) * CH)
            for k in range(FM):
                w = P if k < FM - 1 else FL
                gb, ab = banks[k_n % 4], banks[(k_n + 1) % 4]
                fg, fa = bk_free[k_n % 4], bk_free[(k_n + 1) % 4]
                m1 = s.step("pe", [xl_ready[g], last["mlp_w"]] + fg, lambda e, k=k, w=w, gb=gb, c=c: e.matmul(
                    gb[0:w, :], w_1[:, FF + k * P:FF + k * P + w], xl[:, c], start=True, stop=True), "up")
                m2 = s.step("pe", fa, lambda e, k=k, w=w, ab=ab, c=c: e.matmul(
                    ab[0:w, :], w_1[:, k * P:k * P + w], xl[:, c], start=True, stop=True), "up")
                gl = gel[k_n // 2 % 2]
                a1 = s.step("act", [m1, last.get(("gel", k_n // 2 % 2))], lambda e, k=k, w=w, gb=gb, gl=gl: e.activation(
                    gl[0:w, :], gb[0:w, :], ACT.Gelu, bias=b_1[0:w, 1, k:k + 1]), "gelu")
                a2 = s.step("dve", [a1, m2, last.get("down_mm")], lambda e, k=k, w=w, ab=ab, gl=gl: e.scalar_tensor_tensor(
                    out=hid[0:w, k, :], in0=ab[0:w, :], scalar=b_1[0:w, 0, k:k + 1], in1=gl[0:w, :],
                    op0=ALU.add, op1=ALU.mult), "hid")
                last[("gel", k_n // 2 % 2)] = a2
                bk_free[k_n % 4], bk_free[(k_n + 1) % 4] = [a1], [a2]
                k_n += 2
            last["up_mm"], last["gelu"], last["xl"] = m2, a1, m2
            yb = SB[:, g % 2, :]
            def down(e, yb=yb):
                for k in range(FM):
                    w = P if k < FM - 1 else FL
                    ins = e.matmul(yb, w_2[0:w, k, :], hid[0:w, k, :], start=(k == 0), stop=(k == FM - 1))
                return ins
            m = s.step("pe", [a2, last.get("s_read"), last.get(("y", g % 2))], down, "down")
            last["down_mm"] = m
            s.step("dve", [m], lambda e, c=c, yb=yb: e.scalar_tensor_tensor(
                out=x_in[0:64, c], in0=yb[0:64, :], scalar=cols[0:64, 2:3], in1=x_out[0:64, c], op0=ALU.add, op1=ALU.add), "resid2")
            o = slice(g * CH + 1, (g + 1) * CH + 1)
            a = s.step("dve", [], lambda e, o=o, yb=yb: e.scalar_tensor_tensor(
                out=x_in[64:P, o], in0=yb[64:P, :], scalar=cols[64:P, 2:3], in1=x_out[64:P, o], op0=ALU.add, op1=ALU.add), "resid2")
            last[("y", g % 2)] = a
            new.append([a])
        last["ffn_dve"] = a
        last["s_read"] = a
        w_uses.extend([bk_free[1][0], bk_free[3][0]] if len(w_uses) % 2 == 0 else [bk_free[3][0], bk_free[1][0]])
        return new

    load_attn(0)
    load_mlp(0)
    for layer in range(DEPTH):
        rotated, probs, m_pT = {}, {}, {}
        table("natural_log_exp_and_others")
        for i in range(NT + 3):
            new, mid, blk, old = i < NT, 1 <= i <= NT, 2 <= i < NT + 2, i >= 3
            if new:
                qk = [project(i, 0), project(i, 1)]
                m_r = norms(i, qk)
            if old:
                m_o = values(i - 3, m_pT[i - 3])
            if new:
                rotated[i] = rotate(i, qk, m_r)
                n, m = project(i, 2)
                keep_v(i, n, m)
            if blk:
                shift_v(i - 2)
            if mid:
                m_kq = turn(i - 1, rotated[i - 1])
            if blk:
                m_pT[i - 2] = blocks(i - 2, probs[i - 2])
            if old:
                m_res = output(i - 3, m_o)
            if mid:
                probs[i - 1] = score(i - 1, m_kq)
        if layer + 1 < DEPTH:
            load_attn(layer + 1)
        x_ready = mlp(m_res)
        if layer + 1 < DEPTH:
            load_mlp(layer + 1)
    return [x_ready[-1][0], t_uses[-1], t_uses[-2]]


_INS = {"L0_attn_x": "x", "L0_attn_Wq": "Wq", "L0_attn_bq": "bq", "L0_attn_Wk": "Wk", "L0_attn_bk": "bk",
        "L0_attn_Wv": "Wv", "L0_attn_bv": "bv", "L0_attn_Wo": "Wo", "L0_attn_bo": "bo", "L0_attn_U": "U",
        "L0_attn_V": "V", "L0_ffn_Wqkv": "Wqkv", "L0_ffn_q_scale": "q_scale", "L0_ffn_k_scale": "k_scale",
        "L0_ffn_Wo": "Wo2", "L0_ffn_ln_g": "ln_g", "L0_ffn_ln_b": "ln_b", "L0_ffn_W1": "W1", "L0_ffn_b1": "b1",
        "L0_ffn_W2": "W2", "L0_ffn_b2": "b2"}


def kernel(**inputs):
    import concourse.bacc as _bacc
    from concourse.bass_utils import run_bass_kernel_spmd as _run

    nc = _bacc.Bacc("TRN2", target_bir_lowering=False, num_devices=1)
    arrays, args = {}, {}
    for name, short in _INS.items():
        arrays[f"in_{short}"] = np.ascontiguousarray(inputs[name])
    for name, a in tables().items():
        arrays[f"in_{name}"] = a
    for name, a in arrays.items():
        args[name[3:]] = nc.dram_tensor(name, a.shape, mybir.dt.from_np(a.dtype), kind="ExternalInput").ap()
    out = nc.dram_tensor("out", (1, T, P), F32, kind="ExternalOutput").ap()
    build(nc, args, out)
    return _run(nc, [arrays], core_ids=[0]).results[0]["out"]
```

```python
from contextlib import ExitStack

import numpy as np

import concourse.bass as bass
from concourse import mybir

F32 = mybir.dt.float32
BF16 = mybir.dt.bfloat16
F32R = mybir.dt.float32r
ALU = mybir.AluOpType
ACT = mybir.ActivationFunctionType
AX = mybir.AxisListType

P = 128
T = 2048
NT = T // P
CH = 512
NC = T // CH

H = 16
HD = P // H
PARTS = 3
PROD = PARTS * PARTS * HD
MAXROW = 96
VC = 32

DEPTH = 6
DH = 64
INNER = H * DH
WIN = 32
NP = H // 2
FF = int(P * 4 * 2 / 3)
FM = -(-FF // P)
FL = FF - (FM - 1) * P
NEG = -1.0e30


def tables():
    half = np.arange(0, DH, 2, dtype=np.float32)
    inv_freq = (np.float32(1.0) / np.power(np.float32(10000.0), half / np.float32(DH))).astype(np.float32)
    freqs = np.arange(T, dtype=np.float32)[:, None] * inv_freq[None, :]
    freqs = np.concatenate([freqs, freqs], -1).astype(np.float64)
    base = (half.astype(np.float64) + 0.4 * DH) / (1.4 * DH)
    base = np.concatenate([base, base])
    local = (np.arange(T) % P - P // 2) / (WIN // 2)
    scale = base[None, :] ** local[:, None]
    sign = np.where(np.arange(DH) < DH // 2, -1.0, 1.0)[None, :]
    cos, sin = np.cos(freqs), np.sin(freqs) * sign
    lay = lambda a: a.reshape(NT, P, DH).transpose(1, 0, 2)
    rot = np.stack([lay(cos * scale), lay(sin * scale), lay(cos / scale), lay(sin / scale)], 1)
    carry = np.tile(base ** (P / (WIN // 2)), 2)[:, None]
    i, c = np.arange(P)[:, None] % WIN, np.arange(2 * WIN)[None, :]
    ok = (i <= c) & (c <= i + WIN)
    first = ok & ~((np.arange(P)[:, None] < WIN) & (c < WIN))
    mask = np.stack([np.where(first, 0.0, NEG), np.where(ok, 0.0, NEG)], 1)
    ident = np.eye(P)
    f = lambda a: np.ascontiguousarray(a, dtype=np.float32)
    return {"rot": f(rot), "carry": f(carry), "mask": f(mask), "ident": f(ident)}


class Schedule:

    def __init__(self, nc, ctx):
        self.nc, self.ctx = nc, ctx
        self.queues = {"pe": [], "dve": [], "act": [], "pool": [], "sp": []}
        self.counts = {}
        self.sems = {}
        self.pool_last = None

    def sem(self, name):
        if name not in self.sems:
            self.sems[name] = self.ctx.enter_context(self.nc.semaphore(name))
            self.counts[name] = 0
        return name

    def step(self, engine, waits, issue, sem):
        self.sem(sem)
        self.counts[sem] += 1
        mark = (sem, self.counts[sem])
        if engine == "pool":
            waits, self.pool_last = list(waits) + [self.pool_last], mark
        self.queues[engine].append((tuple(waits), issue, sem, 1))
        return mark

    def dma(self, engine, waits, out, in_, sem):
        self.sem(sem)
        self.counts[sem] += 16
        self.queues[engine].append((tuple(waits), lambda e: e.dma_start(out, in_), sem, 16))
        return (sem, self.counts[sem])

    def play(self, engine, e):
        seen = {}
        for waits, issue, sem, inc in self.queues[engine]:
            for mark in waits:
                if mark is not None and seen.get(mark[0], 0) < mark[1]:
                    e.wait_ge(self.sems[mark[0]], mark[1])
                    seen[mark[0]] = mark[1]
            ins = issue(e)
            if inc:
                ins.then_inc(self.sems[sem], inc)


def rsqrt_start(s, name, src, tmp, out, lo, ready):
    c, t = tmp
    op = ALU.max if lo[0] == "max" else ALU.add
    a = s.step("dve", ready, lambda e: e.tensor_scalar(c, src, lo[1], None, op), name + "_arg")
    b = s.step("act", [a], lambda e: e.activation(t, c, ACT.Ln), name + "_ln")
    return a, s.step("act", [b], lambda e: e.activation(out, t, ACT.Exp, scale=-0.5), name + "_exp")


def rsqrt_finish(s, name, tmp, out, m):
    c, t = tmp
    d = s.step("dve", [m], lambda e: e.tensor_tensor(t, out, out, ALU.mult), name + "_sq")
    d = s.step("dve", [d], lambda e: e.scalar_tensor_tensor(
        out=t, in0=t, scalar=-0.5, in1=c, op0=ALU.mult, op1=ALU.mult), name + "_sq")
    return s.step("dve", [d], lambda e: e.scalar_tensor_tensor(
        out=out, in0=t, scalar=1.5, in1=out, op0=ALU.add, op1=ALU.mult), name + "_r")


def build(nc, d, out):
    with ExitStack() as ctx:
        s = Schedule(nc, ctx)
        sb = lambda c, n, shape, dt=F32: c.enter_context(nc.sbuf_tensor(n, shape, dt))
        ps = lambda c, n, shape, dt=F32: c.enter_context(nc.psum_tensor(n, shape, dt))

        y_dram = nc.dram_tensor("y_scratch", (P, T), F32, kind="Internal").ap()
        l_dram = nc.dram_tensor("l_scratch", (P, T), F32, kind="Internal").ap()
        att_dram = nc.dram_tensor("att_scratch", (P, T), F32, kind="Internal").ap()
        stream = [sb(ctx, f"stream{i}", [P, T + 1]) for i in range(2)]
        cut_dram = {n: nc.dram_tensor(n + "_cut", (2,) + tuple(d[n].shape), F32, kind="Internal").ap() for n in ("Wqkv", "W1")}
        early = (sb(ctx, "w_qkv", [P, 2, 3 * INNER], F32R), sb(ctx, "w_o", [P, NP, P]))
        w_out = sb(ctx, "w_out", [P, P])
        bo = sb(ctx, "bo", [P, 1])
        ident = sb(ctx, "ident", [P, P])
        ident_bf = sb(ctx, "ident_bf", [P, P], BF16)
        ones = sb(ctx, "ones", [P, P])
        ones_row = sb(ctx, "ones_row", [1, P])
        carry = sb(ctx, "carry", [P, 1])
        mask_bf = sb(ctx, "mask_bf", [P, 2, NP, 2 * WIN], BF16)

        x_rows = d["x"].rearrange("a (i p) d -> p (a i) d", p=P)
        m_id = s.dma("sp", [], ident[:, :], d["ident"], "ld_id")
        m_tab = s.dma("sp", [], carry[:, :], d["carry"], "ld_tab")

        m_ones = s.step("pool", [], lambda e: e.memset(ones[:, :], 1.0 / P), "const")
        m_ones = s.step("pool", [], lambda e: e.memset(ones_row[:, :], 1.0), "const")
        for i in range(2):
            m_ones = s.step("pool", [], lambda e, i=i: e.memset(stream[i][64:P, 0:1], 0.0), "const")

        def load_early(m_cut):
            w_qkv, w_o = early
            for j in range(3):
                c = slice(j * INNER, (j + 1) * INNER)
                for k in range(2):
                    early_marks["w", j] = s.dma("sp", m_cut, w_qkv[:, k, c].bitcast(F32), cut_dram["Wqkv"][k, 0][:, c], f"ld_wqkv{j}")
            early_marks["w_o"] = s.dma("sp", [], w_o[:, :, :], d["Wo2"][0].rearrange("(k p) n -> p k n", p=P), "ld_wo")

        early_marks = {}
        with ExitStack() as phase_a:
            done_a = part_a(nc, s, phase_a, sb, ps, d, cut_dram, load_early, x_rows, y_dram, l_dram, w_out, bo, stream, ident, ident_bf, ones_row,
                            m_id, m_ones)

        with ExitStack() as phase_b:
            m_out = part_b(nc, s, phase_b, sb, ps, d, stream, ident, ident_bf, ones, ones_row, carry, mask_bf, m_tab,
                           m_ones, done_a, cut_dram, early, early_marks, w_out, bo, y_dram, l_dram, att_dram, x_rows,
                           out.rearrange("a (i p) d -> p (a i) d", p=P))
        sems = s.sems
        block = ctx.enter_context(nc.Block())

        @block.sync
        def _(e):
            s.play("sp", e)
            for name, count in m_out:
                e.wait_ge(sems[name], count)

        @block.gpsimd
        def _(e):
            s.play("pool", e)

        @block.scalar
        def _(e):
            s.play("act", e)

        @block.vector
        def _(e):
            s.play("dve", e)

        @block.tensor
        def _(e):
            s.play("pe", e)


def part_a(nc, s, ctx, sb, ps, d, cut_dram, load_early, x_rows, y_dram, l_dram, w_out, bo, stream, ident, ident_bf, ones_row, m_id, m_ones):
    x_tok = sb(ctx, "x_tok", [P, NT, P])
    m_x = s.dma("sp", [], x_tok[:, :, :], x_rows, "ld_x")
    w_raw = {n: sb(ctx, "w_" + n, [P, P]) for n in ("Wq", "Wk", "Wv", "Wo")}
    b_col = {n: sb(ctx, "b_" + n, [P, 1]) for n in ("bq", "bk", "bv")}
    b_col["bo"] = bo
    bdV = sb(ctx, "bdV", [P, P])
    bdU = sb(ctx, "bdU", [P, P])
    xn_T = sb(ctx, "xn_T", [P, T])
    sq = sb(ctx, "sqA", [P, NT, P])
    stat = sb(ctx, "statA", [P, 6, NT])
    w_z = {n: sb(ctx, "wz_" + n, [P, P]) for n in ("Wq", "Wk", "Wv")}
    b_z = {n: sb(ctx, "bz_" + n, [P, 1]) for n in ("bq", "bk")}
    bv_row = sb(ctx, "bv_row", [1, P])
    wo_T = sb(ctx, "wo_T", [P, P])
    z = {n: sb(ctx, "z_" + n, [P, T]) for n in "qk"}
    zp = {n: sb(ctx, "zp_" + n, [P, PARTS, T], BF16) for n in "qk"}
    va = sb(ctx, "va", [P, NT, H, VC])
    QS = [sb(ctx, f"QS{i}", [P, T], BF16) for i in range(3)]
    KS = [sb(ctx, f"KS{i}", [P, T], BF16) for i in range(3)]
    mx = [sb(ctx, f"mx{i}", [P, NT, 2]) for i in range(2)]
    nmax = [sb(ctx, f"nmax{i}", [P, NT]) for i in range(2)]
    nm_r = sb(ctx, "nm_r", [NT, P])
    nm_p = [sb(ctx, f"nm_p{i}", [NT, PARTS, P], BF16) for i in range(2)]
    NPT = 8
    PT = [sb(ctx, f"PT{i}", [P, CH]) for i in range(NPT)]
    w_raw_b, w_cut_b = sb(ctx, "w_raw_b", [P, CH]), sb(ctx, "w_cut_b", [P, 2, CH], F32R)
    o_h = [sb(ctx, f"o_h{i}", [P, CH]) for i in range(2)]
    S_ps = [ps(ctx, f"S_ps{i}", [P, 2, CH]) for i in range(2)]
    E_ps = [ps(ctx, f"E_ps{i}", [P, CH]) for i in range(2)]
    O_ps = ps(ctx, "O_ps", [P, CH])
    M_ps = ps(ctx, "M_ps", [P, CH])

    for n in w_raw:
        m_w = s.dma("sp", [], w_raw[n][:, :], d[n], "ld_w")
    for n in b_col:
        m_w = s.dma("sp", [], b_col[n][:, :], d[n].rearrange("(p o) -> p o", o=1), "ld_w")
    m_z = s.step("pool", [], lambda e: e.memset(bdV[:, :], 0.0), "zeroA")
    m_z = s.step("pool", [], lambda e: e.memset(bdU[:, :], 0.0), "zeroA")
    for h in range(H):
        b = slice(h * HD, (h + 1) * HD)
        s.dma("sp" if h % 2 else "act", [m_z], bdV[b, b], d["V"], "ld_bd")
        m_bd = s.dma("act" if h % 2 else "sp", [m_z], bdU[b, b], d["U"], "ld_bd")
    m_va = s.step("pool", [], lambda e: e.memset(va[:, :, :, :], 1.0), "zeroA")
    for i in range(3):
        s.step("pool", [], lambda e, i=i: e.memset(QS[i][64:P, :], 0.0), "zeroA")
        m0 = s.step("pool", [], lambda e, i=i: e.memset(KS[i][64:P, :], 0.0), "zeroA")
        m_st = s.step("pool", [m0], lambda e, i=i: e.memset(KS[i][MAXROW:MAXROW + PARTS, :], 1.0), "zeroA")
    m_idb = s.step("dve", [m_id], lambda e: e.tensor_copy(ident_bf[:, :], ident[:, :]), "idb")

    s.queues["act"].append(((), lambda e: e.preload_act_table_set("natural_log_exp_and_others"), None, 0))
    bc = lambda a: a.unsqueeze(2).to_broadcast([P, NT, P])
    mean, var = stat[:, 0, :], stat[:, 1, :]
    a = s.step("dve", [m_x], lambda e: e.tensor_reduce(mean, x_tok[:, :, :], AX.X, ALU.add), "lnA")
    a = s.step("dve", [a], lambda e: e.tensor_scalar(mean, mean, 1.0 / P, None, ALU.mult), "lnA")
    a = s.step("dve", [a], lambda e: e.tensor_tensor(x_tok[:, :, :], x_tok[:, :, :], bc(mean), ALU.subtract), "lnA")
    a = s.step("dve", [a], lambda e: e.tensor_tensor(sq[:, :, :], x_tok[:, :, :], x_tok[:, :, :], ALU.mult), "lnA")
    a = s.step("dve", [a], lambda e: e.tensor_reduce(var, sq[:, :, :], AX.X, ALU.add), "lnA")
    a = s.step("dve", [a], lambda e: e.tensor_scalar(var, var, 1.0 / P, None, ALU.mult), "lnA")
    tmp = (stat[:, 2, :], stat[:, 3, :])
    r = rsqrt_start(s, "rA", var, tmp, stat[:, 4, :], ("add", 1e-5), [a])[1]
    r = rsqrt_finish(s, "rA", tmp, stat[:, 4, :], r)
    m_xn = s.step("dve", [r], lambda e: e.tensor_tensor(sq[:, :, :], x_tok[:, :, :], bc(stat[:, 4, :]), ALU.mult), "lnA")

    scale = 1.0 / float(np.sqrt(np.float32(HD)))
    banks = [S_ps[0][:, 0, :], S_ps[0][:, 1, :], S_ps[1][:, 0, :], S_ps[1][:, 1, :], E_ps[0][:, :], E_ps[1][:, :],
             O_ps[:, :], M_ps[:, :]]
    free = [None] * 8
    turn_n = [0]

    def bank():
        turn_n[0] = (turn_n[0] + 1) % 8
        return turn_n[0]

    def small(waits, mm, evac, sem):
        b = bank()
        m = s.step("pe", waits + [free[b]], lambda e: mm(e, banks[b]), sem + "_mm")
        free[b] = s.step("dve", [m], lambda e: evac(e, banks[b]), sem)
        return free[b]

    for n in ("Wq", "Wk", "Wv"):
        k = scale if n == "Wq" else 1.0
        m_wz = small([m_w, m_bd], lambda e, b, n=n: e.matmul(b[:, 0:P], w_raw[n][:, :], bdV[:, :], start=True, stop=True),
                     lambda e, b, n=n, k=k: e.tensor_scalar(w_z[n][:, :], b[:, 0:P], k, None, ALU.mult), "fold")
    for n in ("bq", "bk"):
        k = scale if n == "bq" else 1.0
        m_wz = small([], lambda e, b, n=n: e.matmul(b[:, 0:1], bdV[:, :], b_col[n][:, :], start=True, stop=True),
                     lambda e, b, n=n, k=k: e.tensor_scalar(b_z[n][:, :], b[:, 0:1], k, None, ALU.mult), "fold")
    m_wz = small([], lambda e, b: e.matmul(b[0:1, 0:P], b_col["bv"][:, :], bdV[:, :], start=True, stop=True),
                 lambda e, b: e.tensor_copy(bv_row[:, :], b[0:1, 0:P]), "fold")
    m_wt = small([m_id], lambda e, b: e.transpose(b[:, 0:P], w_raw["Wo"][:, :], ident[:, :]),
                 lambda e, b: e.tensor_copy(wo_T[:, :], b[:, 0:P]), "fold")
    m_wz = small([m_wt], lambda e, b: e.matmul(b[:, 0:P], bdU[:, :], wo_T[:, :], start=True, stop=True),
                 lambda e, b: e.tensor_copy(w_out[:, :], b[:, 0:P]), "fold")

    for g in range(NC):
        def turn(e, bk, g=g):
            for j in range(4):
                ins = e.transpose(bk[:, j * P:(j + 1) * P], sq[:, 4 * g + j, :], ident[:, :])
            return ins
        b = bank()
        m = s.step("pe", [m_xn, m_id, free[b]], lambda e, b=b, t=turn: t(e, banks[b]), "xT_mm")
        c = slice(g * CH, (g + 1) * CH)
        free[b] = s.step("act", [m], lambda e, b=b, c=c: e.activation(xn_T[:, c], banks[b], ACT.Copy), "xT")
        s.step("pool", [free[b]], lambda e, c=c: e.tensor_copy(stream[0][0:64, c], xn_T[0:64, c]), "skew")
        m_skew = s.step("pool", [], lambda e, c=c, g=g: e.tensor_copy(
            stream[0][64:P, g * CH + 1:(g + 1) * CH + 1], xn_T[64:P, c]), "skew")
        m_xT = free[b]

    m_part = {}
    for n, w, bz in (("q", "Wq", "bq"), ("k", "Wk", "bk")):
        for g in range(NC):
            c = slice(g * CH, (g + 1) * CH)
            b = bank()
            m = s.step("pe", [m_xT, m_wz, free[b]], lambda e, b=b, c=c, w=w: e.matmul(
                banks[b], w_z[w][:, :], xn_T[:, c], start=True, stop=True), "z_mm")
            free[b] = s.step("act", [m], lambda e, b=b, c=c, n=n, bz=bz: e.activation(
                z[n][:, c], banks[b], ACT.Identity, bias=b_z[bz][:, 0:1]), "z")
        a = free[b]
        for i in range(PARTS):
            a = s.step("dve", [a], lambda e, n=n, i=i: e.tensor_copy(zp[n][:, i, :], z[n][:, :]), "part")
            if i < PARTS - 1:
                a = s.step("dve", [a], lambda e, n=n, i=i: e.tensor_tensor(
                    z[n][:, :], z[n][:, :], zp[n][:, i, :], ALU.subtract), "part")
        m_part[n] = a

    for g in range(NC):
        def vals(e, bk, g=g):
            for j in range(4):
                i = 4 * g + j
                e.matmul(bk[:, j * P:(j + 1) * P], xn_T[:, i * P:(i + 1) * P], w_z["Wv"][:, :],
                         start=(j == 0), stop=False, skip_group_check=True)
                ins = e.matmul(bk[:, j * P:(j + 1) * P], ones_row[:, :], bv_row[:, :],
                               start=False, stop=True, skip_group_check=True)
            return ins
        b = bank()
        m = s.step("pe", [free[b], m_ones], lambda e, b=b, f=vals: f(e, banks[b]), "v_mm")
        free[b] = s.step("act", [m, m_va], lambda e, b=b, g=g: e.activation(
            va[:, 4 * g:4 * g + 4, :, 0:HD],
            banks[b].rearrange("p (j h d) -> p j h d", j=4, h=H), ACT.Copy), "va")
        m_vals = free[b]

    m_stack = {}
    m_pass1 = {}
    m_pass2 = {}
    reads = []
    exps = []
    pvs = []
    m_nrow = {}
    m_oev = {}
    m_tr = {}
    m_nmdma = {}
    m_odma = {}

    def stack(h):
        sl = h % 3
        w = [m_st, m_pass2.get(h - 3)]
        rows = slice(h * HD, (h + 1) * HD)
        for i in range(PARTS):
            for j in range(PARTS):
                to = slice((PARTS * i + j) * HD, (PARTS * i + j + 1) * HD)
                s.dma("sp", w + [m_part["q"]], QS[sl][to, :], zp["q"][rows, i, :], f"ld_stack{sl}")
                m_stack[h] = s.dma("sp" if h else "act", w + [m_part["k"]], KS[sl][to, :], zp["k"][rows, j, :], f"ld_stack{sl}")

    def scores(h, i, hf):
        sl, n = h % 3, len(reads)
        def mm(e):
            for c in range(2):
                k = (2 * hf + c) * CH
                ins = e.matmul(S_ps[n % 2][:, c, :], QS[sl][0:MAXROW, i * P:(i + 1) * P],
                               KS[sl][0:MAXROW, k:k + CH], start=True, stop=True)
            return ins
        m = s.step("pe", [m_stack[h], reads[n - 2] if n >= 2 else free_all], mm, "sc_mm")
        reads.append(s.step("dve", [m, m_tr.get(h - 2)], lambda e: e.tensor_reduce(
            mx[h % 2][:, i, hf:hf + 1], S_ps[n % 2][:, :, :], AX.XY, ALU.max), "sc_max"))

    def max_rows(h):
        sl, b = h % 3, h % 2
        a = s.step("dve", [reads[-1]], lambda e: e.tensor_reduce(nmax[b][:, :], mx[b][:, :, :], AX.X, ALU.max, negate=True), "nm")
        m_tr[h] = a
        a = s.step("pe", [a, m_nrow.get(h - 1), m_id], lambda e: e.transpose(M_ps[0:NT, 0:P], nmax[b][:, :], ident[:, :]), "nm_T")
        a = s.step("dve", [a], lambda e: e.tensor_copy(nm_r[:, :], M_ps[0:NT, 0:P]), "nm")
        m_nrow[h] = a
        for i in range(PARTS):
            a = s.step("dve", [a, m_nmdma.get(h - 2)], lambda e, i=i: e.tensor_copy(nm_p[b][:, i, :], nm_r[:, :]), "nm")
            if i < PARTS - 1:
                a = s.step("dve", [a], lambda e, i=i: e.tensor_tensor(nm_r[:, :], nm_r[:, :], nm_p[b][:, i, :], ALU.subtract), "nm")
        for i in range(PARTS):
            m_nmdma[h] = s.dma("sp", [a, m_pass2.get(h - 3)], QS[sl][MAXROW + i:MAXROW + i + 1, :], nm_p[b][:, i, :], f"ld_max{b}")

    def probs(h, j, c):
        sl, n = h % 3, len(exps)
        m = s.step("pe", [m_nmdma[h], exps[n - 2] if n >= 2 else free_all], lambda e: e.matmul(
            E_ps[n % 2][:, :], KS[sl][0:MAXROW + PARTS, j * P:(j + 1) * P],
            QS[sl][0:MAXROW + PARTS, c * CH:(c + 1) * CH], start=True, stop=True), "pr_mm")
        exps.append(s.step("act", [m, pvs[n - NPT] if n >= NPT else None], lambda e: e.activation(
            PT[n % NPT][:, :], E_ps[n % 2][:, :], ACT.Exp), "pr_exp"))
        m_pass2[h] = m

    def values(h, j):
        for c in range(NC):
            n = len(pvs)
            pvs.append(s.step("pe", [exps[n], m_vals, m_oev.get(h - 1)] if j == 0 else [exps[n]],
                              lambda e, c=c, n=n: e.matmul(
                O_ps[VC * c:VC * (c + 1), :], va[:, j, h, :], PT[n % NPT][:, :], start=(j == 0), stop=(j == NT - 1)), "pv"))
        if j == NT - 1:
            b = h % 2
            m_oev[h] = s.step("dve", [pvs[-1], m_odma.get(h - 2)], lambda e: e.tensor_copy(o_h[b][:, :], O_ps[:, :]), "o_ev")
            rows = slice(h * HD, (h + 1) * HD)
            for c in range(NC):
                s.dma("sp", [m_oev[h]], y_dram[rows, c * CH:(c + 1) * CH], o_h[b][VC * c:VC * c + HD, :], f"ld_o{b}")
                m_odma[h] = s.dma("sp", [m_oev[h]], l_dram[rows, c * CH:(c + 1) * CH], o_h[b][VC * c + HD:VC * c + 2 * HD, :], f"ld_o{b}")

    pieces = []
    for n, width in (("Wqkv", CH), ("W1", FF)):
        for layer in range(DEPTH):
            for c in range(0, d[n].shape[2], width):
                pieces.append((n, layer, slice(c, c + width)))
    EVERY = 5
    m_cut = {}
    m_cut_st = []

    def cut_weights(k):
        if 0 < k <= len(pieces):
            n, layer, c = pieces[k - 1]
            for i in range(2):
                m_cut_st.append(s.dma("sp", [m_cut[k - 1]], cut_dram[n][i, layer][:, c], w_cut_b[:, i, 0:c.stop - c.start].bitcast(F32), "st_cut"))
        if k < len(pieces):
            n, layer, c = pieces[k]
            raw, hi, lo = w_raw_b[:, 0:c.stop - c.start], w_cut_b[:, 0, 0:c.stop - c.start], w_cut_b[:, 1, 0:c.stop - c.start]
            a = s.dma("sp", [m_cut.get(k - 1)], raw, d[n][layer][:, c], "ld_cut")
            s.step("pool", [a] + m_cut_st[-1:], lambda e: e.tensor_copy(hi, raw), "cut")
            m_cut[k] = s.step("pool", [], lambda e: e.tensor_tensor(lo, raw, hi, ALU.subtract), "cut")

    assert EVERY * len(pieces) < H * NT
    free_all = s.step("pe", free, lambda e: e.matmul(M_ps[0:1, 0:1], ones_row[0:1, 0:1], ones_row[0:1, 0:1], start=True, stop=True), "prep")
    AHEAD = NT + 2
    stack(0)
    stack(1)
    last_values = None
    for u in range(H * NT + AHEAD):
        n, k = u, u - AHEAD
        mh, mi = divmod(n, NT)
        eh, ej = divmod(k, NT)
        if k >= 0 and ej == 0 and eh + 2 < H:
            stack(eh + 2)
        if n % EVERY == 0:
            cut_weights(n // EVERY)
        if n == H * NT:
            load_early(m_cut_st[-1:])
        for c in range(NC):
            if k >= 0:
                probs(eh, ej, c)
            if mh < H and c % 2 == 0:
                scores(mh, mi, c // 2)
            if last_values and c == 1:
                values(*last_values)
        if mh < H and mi == NT - 1:
            max_rows(mh)
        last_values = (eh, ej) if k >= 0 else None
    values(*last_values)

    return [m_skew, pvs[-1], exps[-1], reads[-1], m_oev[H - 1], m_odma[H - 1], m_odma[H - 2], m_part["k"], m_idb, m_cut_st[-1]]


def part_b(nc, s, ctx, sb, ps, d, stream, ident, ident_bf, ones, ones_row, carry, mask_bf, m_tab, m_ones, done_a,
           cut_dram, early, early_marks, w_out, bo, y_dram, l_dram, att_dram, x_rows, out_rows):
    w_qkv, w_o = early
    w_1 = sb(ctx, "w_1", [P, 2, 2 * FF], F32R)
    rot = [sb(ctx, f"rot{i}", [P, 4, DH]) for i in range(2)]
    x_cut = [sb(ctx, f"x_cut{i}", [P, 2, P], F32R) for i in range(2)]
    w_2 = sb(ctx, "w_2", [P, FM, P])
    b_1 = sb(ctx, "b_1", [P, 2, FM])
    cols = sb(ctx, "cols", [P, 3])
    gains = [sb(ctx, f"gains{i}", [P, 4, DH]) for i in range(2)]
    rt = [sb(ctx, f"rt{i}", [P, 4, DH]) for i in range(2)]
    ss = [sb(ctx, f"ss{i}", [P, 2 * H]) for i in range(2)]
    rs = [[sb(ctx, f"rs{i}{j}", [P, 2 * H]) for j in range(3)] for i in range(2)]
    nrms = [[sb(ctx, f"nrm{i}{j}", [P, INNER]) for i in range(2)] for j in range(2)]
    tcs = [[sb(ctx, f"tc{i}{j}", [P, INNER]) for i in range(2)] for j in range(2)]
    ts = [sb(ctx, f"ts{i}", [P, INNER]) for i in range(2)]
    q_T = sb(ctx, "q_T", [P, NP, P])
    k_T = [sb(ctx, f"k_T{i}", [P, NP, WIN + P]) for i in range(2)]
    NV = 4
    v = [sb(ctx, f"v{i}", [P, INNER]) for i in range(NV)]
    pr = [sb(ctx, f"pr{i}", [P, H, 2 * WIN]) for i in range(2)]
    pc = sb(ctx, "pc", [P, H, 2 * WIN])
    mx = sb(ctx, "mxB", [P, 3, H])
    pT = sb(ctx, "pT", [P, H, P])
    pL = sb(ctx, "pL", [P, H, WIN])
    o_T = sb(ctx, "o_T", [P, NP, P])
    xl = sb(ctx, "xl", [P, CH])
    xl_cut = sb(ctx, "xl_cut", [P, 2, CH], F32R)
    lnb = sb(ctx, "lnb", [P, CH])
    row = sb(ctx, "row", [1, 3, CH])
    hid = sb(ctx, "hid", [P, FM, CH])
    gel = [sb(ctx, f"gel{i}", [P, CH]) for i in range(2)]
    att_c = [sb(ctx, f"att_c{i}", [P, CH]) for i in range(2)]
    x_c = [sb(ctx, f"x_c{i}", [P, CH // P, P]) for i in range(2)]
    W_ps = [ps(ctx, f"W_ps{i}", [P, 2, CH]) for i in range(2)]
    T_ps = [ps(ctx, f"T_ps{i}", [P, CH]) for i in range(2)]
    S_ps = ps(ctx, "SB_ps", [P, 2, NP, 2 * WIN])

    m_mask = s.dma("sp", done_a, lnb[:, 0:4 * WIN], d["mask"].rearrange("p a b -> p (a b)"), "ld_tab")
    m_mask = s.step("dve", [m_mask] + done_a, lambda e: e.tensor_copy(
        mask_bf[:, :, :, :], lnb[:, 0:4 * WIN].rearrange("p (a b) -> p a b", a=2).unsqueeze(2).to_broadcast([P, 2, NP, 2 * WIN])), "mask")
    s.step("pool", done_a, lambda e: e.memset(pT[:, :, :], 0.0), "zeroB")
    for i in range(2):
        m_zero = s.step("pool", [], lambda e, i=i: e.memset(k_T[i][:, :, 0:WIN], 0.0), "zeroB")

    last = dict(early_marks)
    x_in, x_out = stream
    n_w, n_t = [0], [0]
    w_read, t_read = {}, {}

    def w_slot():
        n_w[0] += 1
        n = n_w[0]
        return n, W_ps[n % 2], w_read.get(n - 2)

    def t_slot():
        n_t[0] += 1
        n = n_t[0]
        return n, T_ps[n % 2], t_read.get(n - 2)

    def table(name):
        s.queues["act"].append(((), lambda e: e.preload_act_table_set(name), None, 0))

    def load_qkv(n, u):
        for j in range(3):
            c = slice(j * INNER, (j + 1) * INNER)
            for k in range(2):
                last[("w", j)] = s.dma("sp", [last[("proj", j, u - 1)]], w_qkv[:, k, c].bitcast(F32), cut_dram["Wqkv"][k, n][:, c], f"ld_wqkv{j}")

    def load_o(n):
        last["w_o"] = s.dma("sp", [last.get("y_mm")], w_o[:, :, :], d["Wo2"][n].rearrange("(k p) n -> p k n", p=P), "ld_wo")

    def load_gains(n):
        g, HF = gains[n % 2], DH // 2
        for i, nme in enumerate(("q_scale", "k_scale")):
            row_of = lambda a, b: d[nme][n:n + 1, a:b].to_broadcast([P, b - a])
            w = done_a + [last.get(("gains_use", n % 2))]
            s.dma("sp", w, g[:, 2 * i, :], row_of(0, DH), f"ld_gains{n % 2}")
            s.dma("sp", w, g[:, 2 * i + 1, 0:HF], row_of(HF, DH), f"ld_gains{n % 2}")
            last[("gains", n)] = s.dma("sp", w, g[:, 2 * i + 1, HF:DH], row_of(0, HF), f"ld_gains{n % 2}")

    def load_mlp(n):
        w = done_a + [last.get("down_mm"), last.get("resid2")]
        for k in range(2):
            s.dma("sp", w, w_1[:, k, :].bitcast(F32), cut_dram["W1"][k, n], "ld_mlp")
        s.dma("sp", w, w_2[:, 0:FM - 1, :], d["W2"][n][0:(FM - 1) * P, :].rearrange("(k p) n -> p k n", p=P), "ld_mlp")
        s.dma("sp", w, w_2[0:FL, FM - 1, :], d["W2"][n][(FM - 1) * P:FF, :], "ld_mlp")
        b = d["b1"][n]
        for i in range(2):
            for k in range(FM):
                m, o = (P if k < FM - 1 else FL), i * FF + k * P
                s.dma("sp", w, b_1[0:m, i, k:k + 1], b[o:o + m].rearrange("(p o) -> p o", o=1), "ld_mlp")
        for i, nme in enumerate(("ln_g", "ln_b", "b2")):
            last["mlp_w"] = s.dma("sp", w, cols[:, i:i + 1], d[nme][n].rearrange("(p o) -> p o", o=1), "ld_mlp")

    def place(u):
        layer, i = divmod(u, NT)
        return layer, i, slice(i * P, (i + 1) * P)

    def load_rot(u):
        last[("rot", u)] = s.dma("sp", done_a + [last.get(("rt", u % 2))], rot[u % 2][:, :, :], d["rot"][:, :, u % NT, :], f"ld_rot{u % 2}")

    def cut_x(u):
        layer, i, c = place(u)
        hi, lo = x_cut[u % 2][:, 0, :], x_cut[u % 2][:, 1, :]
        ready = done_a if layer == 0 else [last[("x", layer, i * P // CH)]]
        a = s.step("dve", ready + [last.get(("proj", 2, u - 2))], lambda e: e.tensor_copy(hi, x_in[:, c]), "cut_x")
        last[("cut", u)] = s.step("dve", [a], lambda e: e.tensor_tensor(lo, x_in[:, c], hi, ALU.subtract), "cut_x")

    def cut_product(e, bank, left, right):
        e.matmul(bank, left[0], right[0], start=True, stop=False)
        e.matmul(bank, left[0], right[1], start=False, stop=False)
        return e.matmul(bank, left[1], right[0], start=False, stop=True)

    def project(u, which):
        xc = x_cut[u % 2]
        n, bank, free = w_slot()
        def mm(e):
            for hf in range(2):
                o = which * INNER + hf * CH
                ins = cut_product(e, bank[:, hf, :], [xc[:, k, :] for k in range(2)], [w_qkv[:, k, o:o + CH] for k in range(2)])
            return ins
        m = s.step("pe", [last[("cut", u)], last[("w", which)], free], mm, "proj")
        last[("proj", which, u)] = m
        return n, bank, m

    def squares(u, i, slot):
        n, bank, m = slot
        nrm = nrms[u % 2]
        a = s.step("act", [m, last.get(("nrm", i, u % 2))], lambda e: e.activation(
            nrm[i][:, :].rearrange("p (a b) -> p a b", a=2), bank[:, :, :], ACT.Square), "sq")
        return s.step("dve", [a, last.get(("rs", u % 2))], lambda e: e.tensor_reduce(
            ss[u % 2][:, i * H:(i + 1) * H], nrm[i][:, :].rearrange("p (h d) -> p h d", h=H), AX.X, ALU.add), "ss")

    def norms(u, a):
        r = [b[:, :] for b in rs[u % 2]]
        return r, rsqrt_start(s, "rB", ss[u % 2][:, :], r[0:2], r[2], ("max", 1e-24), [a])[1]

    def normalise(u, qk, r, m_r):
        st, marks, nrm = u % 2, [], nrms[u % 2]
        m_r = rsqrt_finish(s, "rB", r[0:2], r[2], m_r)
        for i, (n, bank, m) in enumerate(qk):
            a = s.step("dve", [m_r], lambda e, i=i, bank=bank: e.tensor_tensor(
                nrm[i][:, :].rearrange("p (h d) -> p h d", h=H), bank[:, :, :].rearrange("p a (h d) -> p (a h) d", d=DH),
                r[2][:, i * H:(i + 1) * H].unsqueeze(2).to_broadcast([P, H, DH]), ALU.mult), "nrm")
            w_read[n] = last[("rs", st)] = a
            marks.append(a)
        return marks

    def rotate(u, marks):
        layer, st, HF = u // NT, u % 2, DH // 2
        tc, nrm = tcs[st], nrms[st]
        view = lambda a: a.rearrange("p (h d) -> p h d", h=H)
        b = lambda t, k: t.unsqueeze(1).to_broadcast([P, H, k])
        m_rt = s.step("pool", [last[("rot", u)], last[("gains", layer)], last.get(("trig", st))], lambda e: e.tensor_tensor(
            rt[st][:, :, :], rot[st][:, :, :], gains[layer % 2][:, :, :], ALU.mult), "rt")
        last[("gains_use", layer % 2)] = last[("rt", st)] = m_rt
        def trig(i, k):
            eng = "dve" if i == 0 else "pool"
            c, sn = rt[st][:, 2 * i, :], rt[st][:, 2 * i + 1, :]
            dst, src, gain, waits = (
                (view(tc[i][:, :]), view(nrm[i][:, :]), b(c, DH), [marks[i], m_rt, last.get(("tc", i, st))]),
                (view(ts[i][:, :])[:, :, 0:HF], view(nrm[i][:, :])[:, :, HF:DH], b(sn[:, 0:HF], HF), [last.get(("ts", i))]),
                (view(ts[i][:, :])[:, :, HF:DH], view(nrm[i][:, :])[:, :, 0:HF], b(sn[:, HF:DH], HF), []))[k]
            return s.step(eng, waits, lambda e: e.tensor_tensor(dst, src, gain, ALU.mult), f"trig{i}")

        def add(i, m):
            last[("nrm", i, st)] = m
            last[("ts", i)] = a = s.step("pool", [m], lambda e: e.tensor_tensor(tc[i][:, :], tc[i][:, :], ts[i][:, :], ALU.add), "rotsum")
            return a

        for k in range(3):
            m = trig(0, k)
        last[("trig", st)] = m
        trig(1, 0)
        q_sum = add(0, m)
        trig(1, 1)
        return [q_sum, add(1, trig(1, 2))]

    def turn(u, rotated, i, hf):
        tc = tcs[u % 2]
        n, bank, free = t_slot()
        tb = bank[:, :].rearrange("p (a b) -> p a b", b=P)
        def tr(e):
            for j in range(4):
                b = 4 * hf + j
                ins = e.transpose(tb[:, j, :], tc[i][:, b * P:(b + 1) * P], ident[:, :])
            return ins
        m = last[("tc", i, u % 2)] = s.step("pe", [rotated[i], free], tr, "turn_mm")
        pair = slice(4 * hf, 4 * hf + 4)
        if i == 0:
            a = s.step("act", [m, last.get("score")], lambda e: e.activation(q_T[:, pair, :], tb, ACT.Copy), "turn")
        else:
            kt, kn = k_T[u % 2], k_T[(u + 1) % 2]
            s.step("act", [m, last.get(("k", u % 2)), m_zero], lambda e: e.activation(
                kt[:, pair, WIN:WIN + P], tb, ACT.Copy), "turn")
            a = s.step("act", [last.get(("k", (u + 1) % 2)), m_tab], lambda e: e.activation(
                kn[:, pair, 0:WIN], tb[:, :, P - WIN:P], ACT.Copy, scale=carry[:, 0:1]), "turn")
        t_read[n] = a
        return a

    def keep_v(u, n, bank, m):
        w_read[n] = last[("v", u)] = s.step("act", [m, last.get(("use", u - NV + 1))], lambda e: e.activation(
            v[u % NV][:, :].rearrange("p (a b) -> p a b", a=2), bank[:, :, :], ACT.Copy), "v")

    def score(u, m_kq):
        kt = k_T[u % 2]
        mk = mask_bf[:, 0 if u % NT == 0 else 1, :, :]
        def mm(e):
            for par in range(2):
                e.matmul(S_ps[:, par, :, :], ident_bf[:, :], mk, start=True, stop=False, skip_group_check=True)
            for p in range(NP):
                for par in range(2):
                    r = slice(DH * par, DH * (par + 1))
                    for w in range(P // WIN):
                        ins = e.matmul(S_ps[WIN * w:WIN * (w + 1), par, p, :], q_T[r, p, WIN * w:WIN * (w + 1)],
                                       kt[r, p, WIN * w:WIN * w + 2 * WIN], start=False, stop=True, skip_group_check=True)
            return ins
        m = s.step("pe", [m_kq, m_mask, last.get("s_read")], mm, "score_mm")
        last["score"] = m
        last[("k", u % 2)] = m
        pb = pr[u % 2]
        sv = S_ps[:, :, :, :].rearrange("p a b c -> p (a b) c")
        bc = lambda a: a.unsqueeze(2).to_broadcast([P, H, 2 * WIN])
        a = s.step("dve", [m], lambda e: e.tensor_reduce(mx[:, 0, :], sv, AX.X, ALU.max), "sm")
        a = s.step("dve", [a, last.get(("pr", u % 2))], lambda e: e.tensor_tensor(pb[:, :, :], sv, bc(mx[:, 0, :]), ALU.subtract), "sm")
        last["s_read"] = a
        return a

    def exps(u, a):
        pb = pr[u % 2]
        return s.step("act", [a], lambda e: e.activation(pb[:, :, :], pb[:, :, :], ACT.Exp, scale=8.0), "smexp")

    def shares(u, a):
        pb = pr[u % 2]
        bc = lambda a: a.unsqueeze(2).to_broadcast([P, H, 2 * WIN])
        a = s.step("dve", [a, last.get("p_norm")], lambda e: e.tensor_reduce(mx[:, 1, :], pb[:, :, :], AX.X, ALU.add), "sm")
        a = s.step("dve", [a], lambda e: e.reciprocal(mx[:, 2, :], mx[:, 1, :]), "sm")
        a = s.step("pool", [a], lambda e: e.tensor_tensor(pb[:, :, :], pb[:, :, :], bc(mx[:, 2, :]), ALU.mult), "pnorm")
        last["p_norm"] = a
        return a

    def blocks(u, m_p):
        pb = pr[u % 2]
        a = s.step("dve", [m_p, last.get("pT")], lambda e: e.transpose(pc[:, :, :], pb[:, :, :]), "pT")
        last[("pr", u % 2)] = a
        return a

    def diagonals(a):
        w = [a, last.get("pv"), m_zero]
        for q in range(P // WIN):
            r = slice(WIN * q, WIN * (q + 1))
            to = slice((r.start - WIN) % P, (r.start - WIN) % P + WIN)
            s.step("act", w, lambda e, r=r: e.activation(pT[r, :, r], pc[r, :, WIN:2 * WIN], ACT.Copy), "pD")
            dst = pT[to, :, r] if q else pL[to, :, :]
            m = s.step("act", w, lambda e, r=r, dst=dst: e.activation(dst, pc[r, :, 0:WIN], ACT.Copy), "pD")
        last["pT"] = m
        return m

    def values(u, m_p, hf):
        n, bank, free = t_slot()
        tb = bank[:, :].rearrange("p (a b) -> p a b", b=P)
        final = slice(P - WIN, P)
        def mm(e):
            for j in range(4):
                for par in range(2):
                    h, at = par * NP + 4 * hf + j, slice(DH * par, DH * (par + 1))
                    f = slice((2 * (4 * hf + j) + par) * DH, (2 * (4 * hf + j) + par + 1) * DH)
                    ins = e.matmul(tb[at, j, :], v[u % NV][:, f], pT[:, h, :], start=(j == 0), stop=(u % NT == 0), skip_group_check=True)
            if u % NT:
                for j in range(4):
                    for par in range(2):
                        h, at = par * NP + 4 * hf + j, slice(DH * par, DH * (par + 1))
                        f = slice((2 * (4 * hf + j) + par) * DH, (2 * (4 * hf + j) + par + 1) * DH)
                        ins = e.matmul(tb[at, j, 0:WIN], v[(u - 1) % NV][final, f], pL[final, h, :],
                                       start=False, stop=True, skip_group_check=True)
            return ins
        m = s.step("pe", [m_p, last[("v", u)], free], mm, "pv_mm")
        a = t_read[n] = s.step("act", [m, last.get("y_mm")], lambda e: e.activation(
            o_T[:, 4 * hf:4 * hf + 4, :], tb, ACT.Copy), "o_T")
        last["pv"] = last[("use", u)] = m
        return a

    def output(u, a):
        layer, i, c = place(u)
        n, bank, free = t_slot()
        def out(e):
            for p in range(NP):
                ins = e.matmul(bank[:, 0:P], w_o[:, p, :], o_T[:, p, :], start=(p == 0), stop=(p == NP - 1))
            return ins
        m = last["y_mm"] = s.step("pe", [a, last["w_o"], free], out, "y_mm")
        w = [m] + [last.get(("x", layer, min(k, NC - 1))) for k in (i * P // CH, i * P // CH + 1)]
        s.step("dve", w, lambda e: e.tensor_tensor(x_out[0:64, c], bank[0:64, 0:P], x_in[0:64, c], ALU.add), "resid")
        o = slice(c.start + 1, c.stop + 1)
        t_read[n] = last[("res", u)] = s.step("dve", [], lambda e: e.tensor_tensor(
            x_out[64:P, o], bank[64:P, 0:P], x_in[64:P, o], ALU.add), "resid")

    mlp = {}

    def ln_mean(layer, g):
        c, x = slice(g * CH, (g + 1) * CH), xl
        n, bank, free = t_slot()
        m = s.step("pe", [last[("res", layer * NT + 4 * g + 3)], free], lambda e: e.matmul(
            bank[:, :], ones[:, :], x_out[:, c], start=True, stop=True), "mean_mm")
        a = t_read[n] = s.step("dve", [m, mlp.get("x"), last["att"]], lambda e: e.tensor_tensor(
            x[:, :], x_out[:, c], bank[:, :], ALU.subtract), "xc")
        mlp["sq"] = s.step("act", [a, last.get("var_mm")], lambda e: e.activation(lnb[:, :], x[:, :], ACT.Square), "lnsq")

    def ln_var(layer, g):
        n, bank, free = t_slot()
        m = last["var_mm"] = s.step("pe", [mlp["sq"], free], lambda e: e.matmul(
            bank[0:1, :], ones[:, 0:1], lnb[:, :], start=True, stop=True), "var_mm")
        t_read[n], mlp["r"] = rsqrt_start(s, "rL", bank[0:1, :], (row[:, 0, :], row[:, 1, :]), row[:, 2, :],
                                          ("add", 1e-5), [m, last.get("bc_mm")])

    def ln_rsqrt():
        mlp["r"] = rsqrt_finish(s, "rL", (row[:, 0, :], row[:, 1, :]), row[:, 2, :], mlp["r"])

    def ln_apply(layer, g):
        x, hi, lo = xl, xl_cut[:, 0, :], xl_cut[:, 1, :]
        n, bank, free = t_slot()
        m = last["bc_mm"] = s.step("pe", [mlp["r"], free], lambda e: e.matmul(
            bank[:, :], ones_row[:, :], row[:, 2, :], start=True, stop=True), "bc_mm")
        a = t_read[n] = s.step("dve", [m], lambda e: e.tensor_tensor(x[:, :], x[:, :], bank[:, :], ALU.mult), "xc")
        a = s.step("dve", [a, last["mlp_w"]], lambda e: e.tensor_scalar(
            x[:, :], x[:, :], cols[:, 0:1], cols[:, 1:2], ALU.mult, ALU.add), "xc")
        a = s.step("act", [a, last.get("up")], lambda e: e.activation(hi, x[:, :], ACT.Copy), "cut_xl")
        mlp["x"] = s.step("dve", [a], lambda e: e.tensor_tensor(lo, x[:, :], hi, ALU.subtract), "cut_xl")

    def up(layer, g, k):
        w, gl = (P if k < FM - 1 else FL), gel[k % 2]
        n, bank, free = w_slot()
        def mm(e):
            for half, o in ((0, FF + k * P), (1, k * P)):
                ins = cut_product(e, bank[0:w, half, :], [w_1[:, i, o:o + w] for i in range(2)], [xl_cut[:, i, :] for i in range(2)])
            return ins
        m = last["up"] = s.step("pe", [mlp["x"], last["mlp_w"], free], mm, "up")
        a = s.step("act", [m, last.get(("gel", k % 2))], lambda e: e.activation(
            gl[0:w, :], bank[0:w, 0, :], ACT.Gelu, bias=b_1[0:w, 1, k:k + 1]), "gelu")
        last[("gel", k % 2)] = w_read[n] = mlp["h"] = s.step("dve", [a, last.get("down_mm"), last["att"]], lambda e: e.scalar_tensor_tensor(
            out=hid[0:w, k, :], in0=bank[0:w, 1, :], scalar=b_1[0:w, 0, k:k + 1], in1=gl[0:w, :],
            op0=ALU.add, op1=ALU.mult), "hid")

    def down(layer, g):
        c = slice(g * CH, (g + 1) * CH)
        n, bank, free = t_slot()
        def mm(e):
            for k in range(FM):
                w = P if k < FM - 1 else FL
                ins = e.matmul(bank[:, :], w_2[0:w, k, :], hid[0:w, k, :], start=(k == 0), stop=(k == FM - 1))
            return ins
        m = last["down_mm"] = s.step("pe", [mlp["h"], free], mm, "down")
        u = layer * NT + min(4 * g + 4, NT - 1)
        s.step("dve", [m, last[("cut", u)], last[("res", layer * NT + 4 * g + 3)]], lambda e: e.scalar_tensor_tensor(
            out=x_in[0:64, c], in0=bank[0:64, :], scalar=cols[0:64, 2:3], in1=x_out[0:64, c], op0=ALU.add, op1=ALU.add), "resid2")
        o = slice(g * CH + 1, (g + 1) * CH + 1)
        t_read[n] = last["resid2"] = last[("x", layer + 1, g)] = s.step("dve", [], lambda e: e.scalar_tensor_tensor(
            out=x_in[64:P, o], in0=bank[64:P, :], scalar=cols[64:P, 2:3], in1=x_out[64:P, o], op0=ALU.add, op1=ALU.add), "resid2")

    att_bufs = [[hid[:, k, :] for k in range(3)], [gel[0][:, :], gel[1][:, :], xl[:, :]]]
    att = {}

    def att_load(g):
        c, w = slice(g * CH, (g + 1) * CH), done_a + [att.get(("mm", g - 2)), att.get(("st", g - 2))]
        s.dma("sp", w, att_bufs[g % 2][0], y_dram[:, c], f"ld_att{g % 2}")
        att["ld", g] = s.dma("sp", w, att_bufs[g % 2][1], l_dram[:, c], f"ld_att{g % 2}")

    def att_norm(g):
        yb, lb, _ = att_bufs[g % 2]
        m = s.step("dve", [att["ld", g]], lambda e: e.reciprocal(lb, lb), "att_norm")
        att["norm", g] = s.step("dve", [m], lambda e: e.tensor_tensor(yb, yb, lb, ALU.mult), "att_norm")

    def att_out(g):
        yb, _, ab = att_bufs[g % 2]
        n, bank, free = t_slot()
        m = s.step("pe", [att["norm", g], free], lambda e: e.matmul(bank[:, :], w_out[:, :], yb, start=True, stop=True), "att_mm")
        att["mm", g] = t_read[n] = s.step("act", [m], lambda e: e.activation(ab, bank[:, :], ACT.Identity, bias=bo[:, 0:1]), "att")
        att["st", g] = last["att"] = s.dma("sp", [att["mm", g]], att_dram[:, g * CH:(g + 1) * CH], ab, f"st_att{g % 2}")

    added = {}

    def fin_load(g):
        w = [added.get(("out", g - 2))] + [att["st", k] for k in range(NC)]
        s.dma("sp", w, att_c[g % 2][:, :], att_dram[:, g * CH:(g + 1) * CH], f"ld_fin{g % 2}")
        added["ld", g] = s.dma("sp", [], x_c[g % 2][:, :, :], x_rows[:, 4 * g:4 * g + 4, :], f"ld_fin{g % 2}")

    def fin_sum(g):
        ac, c, o = att_c[g % 2], slice(g * CH, (g + 1) * CH), slice(g * CH + 1, (g + 1) * CH + 1)
        s.step("dve", [last["x", DEPTH, g], added["ld", g]], lambda e: e.tensor_tensor(
            ac[0:64, :], ac[0:64, :], x_in[0:64, c], ALU.add), "fin_sum")
        added["sum", g] = s.step("dve", [], lambda e: e.tensor_tensor(ac[64:P, :], ac[64:P, :], x_in[64:P, o], ALU.add), "fin_sum")

    def finish(g):
        ac = att_c[g % 2]
        n, bank, free = t_slot()
        tb = bank[:, :].rearrange("p (j f) -> p j f", f=P)
        def turn_back(e):
            for j in range(CH // P):
                ins = e.transpose(tb[:, j, :], ac[:, j * P:(j + 1) * P], ident[:, :])
            return ins
        m = s.step("pe", [added["sum", g], free], turn_back, "fin_T")
        xc = x_c[g % 2][:, :, :]
        m = t_read[n] = s.step("dve", [m], lambda e: e.tensor_tensor(xc, tb, xc, ALU.add), "fin_add")
        added["out", g] = s.dma("sp", [m], out_rows[:, 4 * g:4 * g + 4, :], xc, f"st_out{g % 2}")

    END = DEPTH * NT
    MLP_LAG = 4
    assert FM == 3

    def pieces(u, where):
        for lag in range(MLP_LAG):
            c, r = divmod(u - 3 - lag - 1, 4)
            if r != 3 or not 0 <= c < DEPTH * NC:
                continue
            layer, g = divmod(c, NC)
            if (lag, where) == (0, "mid"):
                ln_mean(layer, g)
                if layer == DEPTH - 1:
                    fin_load(g)
            if (lag, where) == (0, "var"):
                ln_var(layer, g)
            if (lag, where) == (0, "rsqrt"):
                ln_rsqrt()
            if (lag, where) == (1, "mid"):
                ln_apply(layer, g)
            if lag == 1 and where[:4] == "unit":
                k = int(where[4])
                if k == 0:
                    table("gelu_and_others")
                up(layer, g, k)
                if k == FM - 1:
                    table("natural_log_exp_and_others")
            if (lag, where) == (2, "end") and layer == DEPTH - 1:
                fin_sum(g)
            if (lag, where) == (3, "mid") and layer == DEPTH - 1:
                finish(g)
            if (lag, where) == (2, "mid"):
                down(layer, g)
                if g == NC - 1 and layer + 1 < DEPTH:
                    load_mlp(layer + 1)

    table("natural_log_exp_and_others")
    load_gains(0)
    load_mlp(0)
    cut_x(0)
    load_rot(0)
    rotated, scored, probs, m_pT = {}, {}, {}, {}
    for u in range(END + 3 + MLP_LAG + 1):
        new, mid, blk, old = u < END, 1 <= u <= END, 2 <= u < END + 2, 3 <= u < END + 3
        if new:
            if u and u % NT == 0:
                load_qkv(u // NT, u)
            if u % NT == NT // 2 and u // NT + 1 < DEPTH:
                load_gains(u // NT + 1)
            qk = [project(u, 0)]
            squares(u, 0, qk[0])
        if mid:
            turn(u - 1, rotated[u - 1], 0, 0)
        if blk:
            a = exps(u - 2, scored[u - 2])
        if new:
            qk.append(project(u, 1))
            m_ss = squares(u, 1, qk[1])
        if blk:
            probs[u - 2] = shares(u - 2, a)
        if mid:
            turn(u - 1, rotated[u - 1], 0, 1)
        if old:
            values(u - 3, m_pT[u - 3], 0)
        if mid:
            turn(u - 1, rotated[u - 1], 1, 0)
        if new:
            r, m_r = norms(u, m_ss)
        if old:
            m_o = values(u - 3, m_pT[u - 3], 1)
        if mid:
            m_kq = turn(u - 1, rotated[u - 1], 1, 1)
        if new:
            m_n = normalise(u, qk, r, m_r)
        if 0 <= u - 3 < NC:
            att_out(u - 3)
        pieces(u, "mid")
        gelus = u >= 8 and u % 4 == 0
        if blk and not gelus:
            m_b = blocks(u - 2, probs[u - 2])
        if new:
            rotated[u] = rotate(u, m_n)
            keep_v(u, *project(u, 2))
        if blk and not gelus:
            m_pT[u - 2] = diagonals(m_b)
        if u + 1 < END:
            cut_x(u + 1)
            load_rot(u + 1)
        if old:
            output(u - 3, m_o)
            if (u - 3) % NT == NT - 1 and (u - 3) // NT + 1 < DEPTH:
                load_o((u - 3) // NT + 1)
        pieces(u, "var")
        pieces(u, "unit0")
        pieces(u, "unit1")
        pieces(u, "unit2")
        if blk and gelus:
            m_pT[u - 2] = diagonals(blocks(u - 2, probs[u - 2]))
        if mid:
            scored[u - 1] = score(u - 1, m_kq)
        pieces(u, "rsqrt")
        pieces(u, "end")
        if 0 <= u - 2 < NC:
            att_norm(u - 2)
        if 0 <= u - 1 < NC:
            att_load(u - 1)
    return [added["out", g] for g in range(NC)]


_INS = {"L0_attn_x": "x", "L0_attn_Wq": "Wq", "L0_attn_bq": "bq", "L0_attn_Wk": "Wk", "L0_attn_bk": "bk",
        "L0_attn_Wv": "Wv", "L0_attn_bv": "bv", "L0_attn_Wo": "Wo", "L0_attn_bo": "bo", "L0_attn_U": "U",
        "L0_attn_V": "V", "L0_ffn_Wqkv": "Wqkv", "L0_ffn_q_scale": "q_scale", "L0_ffn_k_scale": "k_scale",
        "L0_ffn_Wo": "Wo2", "L0_ffn_ln_g": "ln_g", "L0_ffn_ln_b": "ln_b", "L0_ffn_W1": "W1", "L0_ffn_b1": "b1",
        "L0_ffn_W2": "W2", "L0_ffn_b2": "b2"}


def kernel(**inputs):
    import concourse.bacc as _bacc
    from concourse.bass_utils import run_bass_kernel_spmd as _run

    nc = _bacc.Bacc("TRN2", target_bir_lowering=False, num_devices=1)
    arrays, args = {}, {}
    for name, short in _INS.items():
        arrays[f"in_{short}"] = np.ascontiguousarray(inputs[name])
    for name, a in tables().items():
        arrays[f"in_{name}"] = a
    for name, a in arrays.items():
        args[name[3:]] = nc.dram_tensor(name, a.shape, mybir.dt.from_np(a.dtype), kind="ExternalInput").ap()
    out = nc.dram_tensor("out", (1, T, P), F32, kind="ExternalOutput").ap()
    build(nc, args, out)
    return _run(nc, [arrays], core_ids=[0]).results[0]["out"]
```
